# Optimizing a Trainium2 kernel written in Bass

```python
import numpy as np
import jax
import jax.numpy as jnp

def _softmax(x, axis=-1):
    return jax.nn.softmax(x, axis=axis)

def _gelu(x):
    return jax.nn.gelu(x, approximate=True)

def _silu(x):
    return jax.nn.silu(x)

def _sigmoid(x):
    return jax.nn.sigmoid(x)

def _layernorm(x, axis=-1, eps=1e-05):
    m = jnp.mean(x, axis=axis, keepdims=True)
    v = jnp.var(x, axis=axis, keepdims=True)
    return (x - m) / jnp.sqrt(v + eps)

def _scatter_add(tgt, idx, src, axis=0):
    return tgt.at[idx].add(src)

def _segment_sum(src, seg, n):
    return jax.ops.segment_sum(src, seg, n)
kernel_name = 'mk_rec_standalone_d1_rec_r8_c1280c'

def setup_inputs(seed: int=0):
    np.random.seed(seed)
    _w = jnp.asarray

    def _rec_inputs():
        import jax
        import jax.numpy as jnp
        _rk = jax.random.key(seed)
        r_users = jax.random.randint(jax.random.fold_in(_rk, 1), (1024,), 72, 99964, jnp.int32)
        r_items = jax.random.randint(jax.random.fold_in(_rk, 2), (1024,), 69, 199973, jnp.int32)
        return (r_users, r_items)
    r_users, r_items = _rec_inputs()

    def _L0_rec_setup():
        import jax, jax.numpy as jnp
        import numpy as np
        N_USERS = 12500
        N_ITEMS = 25000
        N_NODES = N_USERS + N_ITEMS
        NNZ = 375000
        DIM = 64
        LM_DIM = 64
        M_PHI = 1000
        N_LAYERS = 3
        SELECTED_K = 1000
        BATCH = 1024

        def _l2norm(x, eps=1e-12):
            return x / jnp.maximum(jnp.linalg.norm(x, axis=1, keepdims=True), eps)

        def _spmm(rows, cols, vals, x):
            return jax.ops.segment_sum(vals[:, None] * x[cols], rows, num_segments=N_NODES)
        key = jax.random.key(seed)
        ks = jax.random.split(key, 12)
        users = jax.random.randint(ks[0], (BATCH,), 0, N_USERS, dtype=jnp.int32)
        items = jax.random.randint(ks[1], (BATCH,), 0, N_ITEMS, dtype=jnp.int32)
        user_emb = 0.1 * jax.random.normal(ks[2], (N_USERS, DIM), jnp.float32)
        item_emb = 0.1 * jax.random.normal(ks[3], (N_ITEMS, DIM), jnp.float32)
        rows = jax.random.randint(ks[4], (NNZ,), 0, N_NODES, dtype=jnp.int32)
        cols = jax.random.randint(ks[5], (NNZ,), 0, N_NODES, dtype=jnp.int32)
        vals = jax.random.uniform(ks[6], (NNZ,), jnp.float32) * 0.1
        phi3 = jax.random.normal(ks[7], (N_USERS, DIM), jnp.float32) * 0.05
        phi4 = jax.random.normal(ks[8], (DIM, M_PHI), jnp.float32) * 0.05
        phi2 = jax.random.normal(ks[9], (N_USERS, M_PHI), jnp.float32) * 0.05
        user_lm_T = _l2norm(jax.random.normal(ks[10], (M_PHI, LM_DIM), jnp.float32))
        item_lm = _l2norm(jax.random.normal(ks[11], (N_ITEMS, LM_DIM), jnp.float32))
        return {'users': users, 'items': items, 'user_emb': user_emb, 'item_emb': item_emb, 'rows': rows, 'cols': cols, 'vals': vals, 'phi3': phi3, 'phi4': phi4, 'phi2': phi2, 'user_lm_T': user_lm_T, 'item_lm': item_lm}
    _L0_rec_all = _L0_rec_setup()
    _L0_rec_in = {k: v for k, v in _L0_rec_all.items() if k in ('user_emb', 'item_emb', 'rows', 'cols', 'vals', 'phi3', 'phi4', 'phi2', 'user_lm_T', 'item_lm')}
    del _L0_rec_all
    return {'r_users': r_users, 'r_items': r_items, 'L0_rec_user_emb': _L0_rec_in['user_emb'], 'L0_rec_item_emb': _L0_rec_in['item_emb'], 'L0_rec_rows': _L0_rec_in['rows'], 'L0_rec_cols': _L0_rec_in['cols'], 'L0_rec_vals': _L0_rec_in['vals'], 'L0_rec_phi3': _L0_rec_in['phi3'], 'L0_rec_phi4': _L0_rec_in['phi4'], 'L0_rec_phi2': _L0_rec_in['phi2'], 'L0_rec_user_lm_T': _L0_rec_in['user_lm_T'], 'L0_rec_item_lm': _L0_rec_in['item_lm']}

def reference(r_users, r_items, L0_rec_user_emb, L0_rec_item_emb, L0_rec_rows, L0_rec_cols, L0_rec_vals, L0_rec_phi3, L0_rec_phi4, L0_rec_phi2, L0_rec_user_lm_T, L0_rec_item_lm):
    import jax
    import jax.numpy as jnp

    def _L0_rec_ref(users, items, user_emb, item_emb, rows, cols, vals, phi3, phi4, phi2, user_lm_T, item_lm):
        import jax, jax.numpy as jnp
        import numpy as np
        N_USERS = 12500
        N_ITEMS = 25000
        N_NODES = N_USERS + N_ITEMS
        NNZ = 375000
        DIM = 64
        LM_DIM = 64
        M_PHI = 1000
        N_LAYERS = 3
        SELECTED_K = 1000
        BATCH = 1024

        def _l2norm(x, eps=1e-12):
            return x / jnp.maximum(jnp.linalg.norm(x, axis=1, keepdims=True), eps)

        def _spmm(rows, cols, vals, x):
            return jax.ops.segment_sum(vals[:, None] * x[cols], rows, num_segments=N_NODES)
        all_emb = jnp.concatenate([user_emb, item_emb], axis=0)
        acc = all_emb
        e = all_emb
        for _ in range(N_LAYERS):
            e = _spmm(rows, cols, vals, e)
            acc = acc + e
        light_out = acc / (N_LAYERS + 1)
        users_id_emb = light_out[:N_USERS]
        items_id_emb = light_out[N_USERS:]
        k = SELECTED_K
        phi1 = phi3 @ phi4
        ulm_t = user_lm_T[:k]
        user_lm = 0.1 * (phi1[:, :k] @ ulm_t) + 0.9 * (phi2[:, :k] @ ulm_t)
        gamma_id = jnp.sum(users_id_emb[users] * items_id_emb[items], axis=1)
        gamma_lm = jnp.sum(user_lm[users] * item_lm[items], axis=1)
        return 0.5 * gamma_id + gamma_lm
    y = _L0_rec_ref(r_users, r_items, L0_rec_user_emb, L0_rec_item_emb, L0_rec_rows, L0_rec_cols, L0_rec_vals, L0_rec_phi3, L0_rec_phi4, L0_rec_phi2, L0_rec_user_lm_T, L0_rec_item_lm)
    return y

_drawn_inputs = setup_inputs


def setup_inputs(seed=0):
    import zlib

    import numpy as np

    out = dict(_drawn_inputs(seed))
    spreads = {}
    factors = {'L0_rec_user_emb': 5.663,
     'L0_rec_item_emb': 4.475,
     'L0_rec_vals': 8.0,
     'L0_rec_phi3': 3.19,
     'L0_rec_phi4': 5.081}
    for name, (base, spread) in spreads.items():
        noise = np.random.default_rng([zlib.crc32(name.encode()), seed]).standard_normal(out[name].shape)
        drawn = base * np.exp(spread * noise) if base else spread * noise
        out[name] = jnp.asarray(drawn.astype(out[name].dtype))
    for name, factor in factors.items():
        out[name] = (out[name] * factor).astype(out[name].dtype)
    return out
```

```python
import numpy as np
import concourse.bass as bass
from concourse import mybir
from contextlib import ExitStack

"""LightGCN propagation (three sparse matrix products) and batch scores.

The edges are sorted on the chip by the 128-node block of their row (a counting sort: a histogram, then
each edge's rank by one-hot matrix products, then an indirect scatter).  A layer then walks the sorted
edges in chunks of 128 that all lie in one block: GpSimd gathers the chunk's source rows, TensorE
multiplies them with a [edge, row-in-block] matrix that holds the edge's value (its product sums the edges
of each row), and VectorE adds the product to the block's accumulator in SBUF.

Node n is at partition n % 128, block n // 128 on chip, and at row (n % 128) * BUCKETS + n // 128 of the
embedding tables in DRAM, so that the accumulators go out in one contiguous run per partition.
"""


def rec_kernel(nc, r_users, r_items, user_emb, item_emb, rows, cols, vals, phi3, phi4, phi2, user_lm_T,
               item_lm, out):
    f32, f16, i32 = mybir.dt.float32, mybir.dt.float16, mybir.dt.int32
    ALU = mybir.AluOpType
    ACT = mybir.ActivationFunctionType
    AX = mybir.AxisListType

    P = 128
    N_USERS, DIM = user_emb.shape
    N_ITEMS = item_emb.shape[0]
    N_NODES = N_USERS + N_ITEMS
    NNZ = rows.shape[0]
    BATCH = r_users.shape[0]
    M_PHI = phi2.shape[1]
    LAYERS = 3

    BLOCKS = -(-N_NODES // P)
    BUCKETS = BLOCKS + 1
    STREAMS = 5
    FULL = NNZ // P
    TAIL = NNZ - FULL * P
    SCOLS = -(-(FULL + 1) // (2 * STREAMS)) * 2
    COLS = SCOLS * STREAMS
    SBODIES = SCOLS // 2
    HALF = 8
    CHUNKS = -(-((COLS * P + BUCKETS * (P - 1)) // P) // (2 * HALF)) * 2 * HALF
    BODIES = CHUNKS // (2 * HALF)
    MAPCOLS = -(-CHUNKS // P)
    GROUPS = BATCH // P
    KT = 8
    CREDIT = 1
    KS = M_PHI // KT

    tables = [nc.dram_tensor(f"table{l}", (P * BUCKETS, DIM), f32, kind="Internal").ap() for l in range(LAYERS + 1)]
    sorted_dram = nc.dram_tensor("sorted_edges", (P * CHUNKS, 3), f32, kind="Internal").ap()
    map_dram = nc.dram_tensor("chunk_map", (MAPCOLS * P,), i32, kind="Internal").ap()

    ctx = ExitStack()
    with ctx:
        def sb(name, shape, dt=f32):
            return ctx.enter_context(nc.sbuf_tensor(name, shape, dt))

        def pb(name, shape, dt=f32):
            return ctx.enter_context(nc.psum_tensor(name, shape, dt))

        def sem(name):
            return ctx.enter_context(nc.semaphore(name))

        acc = sb("acc", [P, BUCKETS * DIM])
        raw_rows = acc[:, 0:COLS].bitcast(i32)
        raw_cols = acc[:, COLS:2 * COLS].bitcast(i32)
        raw_vals = acc[:, 2 * COLS:3 * COLS]
        scratch_i = acc[:, 3 * COLS:4 * COLS].bitcast(i32)
        hi = acc[:, 4 * COLS:5 * COLS]
        rec = sb("rec", [P, COLS, 3])
        rec_s = rec[:, :, :].rearrange("p (s c) f -> p s c f", s=STREAMS)
        srt = sb("srt", [P, CHUNKS, 3])
        phi2_g = srt[:, :, :].rearrange("p c f -> p (c f)")[:, 0:GROUPS * M_PHI].rearrange("p (g m) -> p g m", g=GROUPS)

        free_words = [0]

        def late(shape):
            width = int(np.prod(shape[1:]))
            at = free_words[0]
            free_words[0] += width
            assert free_words[0] <= COLS * 3
            flat = rec[:, :, :].rearrange("p c f -> p (c f)")[0:shape[0], at:at + width]
            if len(shape) == 2:
                return flat
            names = "abc"[:len(shape) - 1]
            return flat.rearrange(f"p ({' '.join(names)}) -> p {' '.join(names)}", **dict(zip(names, shape[1:])))

        iota_i = sb("iota_i", [P, BUCKETS], i32)
        iota_b = sb("iota_b", [P, BUCKETS], f16)
        iota_r = sb("iota_r", [P, P])
        tmap_i = sb("tmap_i", [P, MAPCOLS], i32)
        tmap = sb("tmap", [P, MAPCOLS])
        ident = sb("ident", [P, P])
        ones = sb("ones", [P, P], f16)
        below = sb("below", [P, P], f16)
        rest = sb("rest", [P, P], f16)
        onehot = sb("onehot", [P, 2, STREAMS, BUCKETS], f16)
        picked = sb("picked", [P, BUCKETS])
        pos = sb("pos", [P, 2, STREAMS])
        pos_i = sb("pos_i", [P, 2, STREAMS], i32)
        pos_lo = sb("pos_lo", [P, 2, STREAMS], i32)
        pos_hi = sb("pos_hi", [P, 2, STREAMS], i32)
        pos_out = sb("pos_out", [P, 2, STREAMS], i32)
        rec_out = sb("rec_out", [P, 2, STREAMS, 3])
        base = sb("base", [P, STREAMS + 1, BUCKETS])
        cnt = sb("cnt", [P, BUCKETS])
        cnt_i = sb("cnt_i", [P, BUCKETS], i32)
        nch_i = sb("nch_i", [P, BUCKETS], i32)
        nch = sb("nch", [P, BUCKETS])
        ends = sb("ends", [P, BUCKETS])
        zero_b = sb("zero_b", [P, BUCKETS])
        blk = sb("blk", [P, MAPCOLS])
        blk_i = sb("blk_i", [P, MAPCOLS], i32)
        chunk_map = sb("chunk_map_sb", [1, MAPCOLS * P], i32)
        idx = sb("idx", [P, 2, HALF], i32)
        got = late([P, 2, HALF, DIM])
        sel = late([P, 2, HALF, P])

        r_i = sb("r_i", [P, 2, GROUPS], i32)
        r_f = sb("r_f", [P, 2, GROUPS])
        r_neg = sb("r_neg", [P, 2, GROUPS])
        r_c = sb("r_c", [P, 2, GROUPS])
        r_idx = sb("r_idx", [P, 2, GROUPS], i32)
        n_i = sb("n_i", [P, 2, GROUPS], i32)
        n_lo = sb("n_lo", [P, 2, GROUPS], i32)
        n_hi = sb("n_hi", [P, 2, GROUPS], i32)
        t_idx = sb("t_idx", [P, 2, GROUPS], i32)
        phi3_g = sb("phi3_g", [P, GROUPS, DIM])
        ilm_g = sb("ilm_g", [P, GROUPS, DIM])
        phi4_sb = sb("phi4_sb", [DIM, M_PHI])
        ulm = sb("ulm", [KS, KT, DIM])
        phi4T = late([KS, KT, DIM])
        w1 = late([DIM, DIM])
        ulm9 = late([KS, KT, DIM])
        featT = late([P, KT + 1, P])
        user_lm = late([P, GROUPS, DIM])
        gamma_lm = sb("gamma_lm", [P, GROUPS])
        gamma_id = sb("gamma_id", [P, GROUPS])
        result = sb("result", [P, GROUPS])
        light = late([P, 2 * GROUPS, DIM])
    
        banks = [pb(f"bank{i}", [P, 512]) for i in range(8)]
        count = [banks[s][:, 0:BUCKETS] for s in range(STREAMS)]

        s_load = sem("s_load")
        s_tab0 = sem("s_tab0")
        s_batch = sem("s_batch")
        s_lmw = sem("s_lmw")
        s_const = sem("s_const")
        s_vconst = sem("s_vconst")
        s_tail = sem("s_tail")
        s_prep = sem("s_prep")
        s_records = sem("s_records")
        s_ridx = sem("s_ridx")
        s_lmg = sem("s_lmg")
        s_hoh = [sem(f"s_hoh{h}") for h in range(2)]
        s_hused = [sem(f"s_hused{h}") for h in range(2)]
        s_zsrt = sem("s_zsrt")
        s_base = sem("s_base")
        s_roh = [sem(f"s_roh{h}") for h in range(2)]
        s_rank = [sem(f"s_rank{h}") for h in range(2)]
        s_read = [sem(f"s_read{h}") for h in range(2)]
        s_rused = [sem(f"s_rused{h}") for h in range(2)]
        s_recs = [sem(f"s_recs{h}") for h in range(2)]
        s_pos = [sem(f"s_pos{h}") for h in range(2)]
        s_pc = sem("s_pc")
        s_scat = [sem(f"s_scat{h}") for h in range(2)]
        s_mapo = sem("s_mapo")
        s_map = sem("s_map")
        s_srt = sem("s_srt")
        s_idx = [[sem(f"s_idx{l}{h}") for h in range(2)] for l in range(LAYERS)]
        s_got = [[sem(f"s_got{l}{h}") for h in range(2)] for l in range(LAYERS)]
        s_sel = [[sem(f"s_sel{l}{h}") for h in range(2)] for l in range(LAYERS)]
        s_prod = [[sem(f"s_prod{l}{h}") for h in range(2)] for l in range(LAYERS)]
        s_free = [[sem(f"s_free{l}{h}") for h in range(2)] for l in range(LAYERS)]
        s_zacc = sem("s_zacc")
        s_add = sem("s_add")
        s_tab = sem("s_tab")
        s_fin = sem("s_fin")
        s_light = sem("s_light")
        s_ft = sem("s_ft")
        s_ftc = sem("s_ftc")
        s_lm = sem("s_lm")
        s_lmc = sem("s_lmc")
        s_out = sem("s_out")

        block = ctx.enter_context(nc.Block())
        U0 = N_USERS // P
        UR = N_USERS - U0 * P
        I0 = P - UR
        IB = (N_ITEMS - I0) // P
        IR = N_ITEMS - I0 - IB * P

        @block.sync
        def _(sp):
            sp.wait_ge(s_tail, 3)
            for raw, dram in ((raw_rows, rows), (raw_cols, cols), (raw_vals, vals)):
                sp.dma_start(raw[:, 0:FULL], dram[0:FULL * P].rearrange("(p n) -> p n", p=P)).then_inc(s_load, 16)
                sp.dma_start(raw[0:TAIL, FULL:FULL + 1], dram[FULL * P:NNZ].rearrange("(p n) -> p n", n=1)).then_inc(s_load, 16)
            sp.dma_start(r_i[:, 0, :], r_users.rearrange("(p g) -> p g", g=GROUPS)).then_inc(s_batch, 16)
            sp.dma_start(r_i[:, 1, :], r_items.rearrange("(p g) -> p g", g=GROUPS)).then_inc(s_batch, 16)
            sp.dma_start(phi4_sb[:, :], phi4).then_inc(s_lmw, 16)
            sp.dma_start(ulm[:, :, :], user_lm_T.rearrange("(c k) d -> k c d", k=KS)).then_inc(s_lmw, 16)
            sp.wait_ge(s_vconst, 1)
            sp.dma_start(sorted_dram.rearrange("(p c) f -> p (c f)", p=P),
                         srt[:, :, :].rearrange("p c f -> p (c f)")).then_inc(s_zsrt, 16)
            t0 = tables[0].rearrange("(p b) d -> p b d", p=P)
            sp.dma_start(t0[:, 0:U0, :], user_emb[0:U0 * P, :].rearrange("(b p) d -> p b d", p=P)).then_inc(s_tab0, 16)
            sp.dma_start(t0[0:UR, U0, :], user_emb[U0 * P:N_USERS, :]).then_inc(s_tab0, 16)
            sp.dma_start(t0[UR:P, U0, :], item_emb[0:I0, :]).then_inc(s_tab0, 16)
            sp.dma_start(t0[:, U0 + 1:U0 + 1 + IB, :], item_emb[I0:I0 + IB * P, :].rearrange("(b p) d -> p b d", p=P)).then_inc(s_tab0, 16)
            sp.dma_start(t0[0:IR, U0 + 1 + IB, :], item_emb[I0 + IB * P:N_ITEMS, :]).then_inc(s_tab0, 16)
            zeros = srt[:, :, :].rearrange("p c f -> p (c f)")[:, 0:DIM]
            sp.dma_start(t0[IR:P, U0 + 1 + IB, :], zeros[IR:P, :]).then_inc(s_tab0, 16)
            sp.dma_start(t0[:, BLOCKS, :], zeros).then_inc(s_tab0, 16)
            sp.wait_ge(s_mapo, 1)
            sp.dma_start(map_dram.rearrange("(p j) -> p j", p=P), blk_i[:, :]).then_inc(s_map, 16)
            sp.wait_ge(s_map, 16)
            sp.dma_start(chunk_map[0:1, :], map_dram.rearrange("(a n) -> a n", a=1)).then_inc(s_map, 16)
            for h in range(2):
                sp.wait_ge(s_scat[h], 16 * STREAMS * SBODIES)
            sp.wait_ge(s_tab0, 112)
            sp.dma_start(srt[:, :, :].rearrange("p c f -> p (c f)"),
                         sorted_dram.rearrange("(p c) f -> p (c f)", p=P)).then_inc(s_srt, 16)
            for l in range(LAYERS):
                sp.wait_ge(s_add, CREDIT + CHUNKS * (l + 1))
                sp.dma_start(tables[l + 1].rearrange("(p b) d -> p (b d)", p=P), acc[:, :]).then_inc(s_tab, 16)
            sp.wait_ge(s_fin, 1)
            sp.dma_start(out.rearrange("(p g) -> p g", g=GROUPS), result[:, :]).then_inc(s_out, 16)
            sp.wait_ge(s_out, 16)

        @block.gpsimd
        def _(pool):
            pool.iota(iota_i[:, :], pattern=[[1, BUCKETS]], base=0, channel_multiplier=0).then_inc(s_const, 1)
            pool.iota(tmap_i[:, :], pattern=[[1, MAPCOLS]], base=0, channel_multiplier=MAPCOLS).then_inc(s_const, 1)
            pool.memset(ones[:, :], 1.0).then_inc(s_const, 1)
            pool.memset(ident[:, :], 0.0).then_inc(s_const, 1)
            pool.wait_ge(s_const, 4)
            pool.affine_select(out=ident[:, :], in_=ident[:, :], compare_op=ALU.not_equal, fill=1.0,
                               base=0, pattern=[[-1, P]], channel_multiplier=1).then_inc(s_const, 1)
            pool.affine_select(out=below[:, :], in_=ones[:, :], compare_op=ALU.is_gt, fill=0.0,
                               base=0, pattern=[[1, P]], channel_multiplier=-1).then_inc(s_const, 1)
            pool.affine_select(out=rest[:, :], in_=ones[:, :], compare_op=ALU.is_ge, fill=0.0,
                               base=0, pattern=[[-1, P]], channel_multiplier=1).then_inc(s_const, 1)
            pool.wait_ge(s_ridx, 1)
            for g in range(GROUPS):
                for dst, src, side in ((phi3_g[:, g, :], phi3, 0), (ilm_g[:, g, :], item_lm, 1)):
                    pool.indirect_dma_start(dst, None, src, bass.IndirectOffsetOnAxis(r_idx[:, side, g:g + 1], 0))\
                        .then_inc(s_lmg, 16)
            pool.wait_ge(s_zsrt, 16)
            with pool.Fori(0, SBODIES) as i:
                for h in range(2):
                    pool.wait_ge(s_recs[h], i + 1)
                    pool.wait_ge(s_pos[h], i + 1)
                    pool.nop(nofuse=True)
                    for s in range(STREAMS):
                        pool.indirect_dma_start(sorted_dram, bass.IndirectOffsetOnAxis(pos_out[:, h, s:s + 1], 0),
                                                rec_out[:, h, s, :], None).then_inc(s_scat[h], 16)
            pool.wait_ge(s_tab0, 112)
            for l in range(LAYERS):
                if l:
                    pool.wait_ge(s_tab, 16 * l)
                with pool.Fori(0, BODIES) as k:
                    for h in range(2):
                        pool.wait_ge(s_idx[l][h], k + 1)
                        pool.nop(nofuse=True)
                        for j in range(HALF):
                            pool.indirect_dma_start(got[:, h, j, :], None, tables[l],
                                                    bass.IndirectOffsetOnAxis(idx[:, h, j:j + 1], 0))\
                                .then_inc(s_got[l][h], 16)
            pool.wait_ge(s_add, CREDIT + CHUNKS * LAYERS)
            for g in range(GROUPS):
                pool.indirect_dma_start(phi2_g[:, g, :], None, phi2,
                                        bass.IndirectOffsetOnAxis(r_idx[:, 0, g:g + 1], 0)).then_inc(s_lmg, 16)
            pool.wait_ge(s_tab, 16 * LAYERS)
            for l in range(LAYERS + 1):
                for side in range(2):
                    for g in range(GROUPS):
                        pool.indirect_dma_start(acc[:, ((l * 2 + side) * GROUPS + g) * DIM:((l * 2 + side) * GROUPS + g + 1) * DIM],
                                                None, tables[l],
                                                bass.IndirectOffsetOnAxis(t_idx[:, side, g:g + 1], 0)).then_inc(s_light, 16)

        @block.scalar
        def _(act):
            act.wait_ge(s_records, 1)

            def stage_records(i, h, first):
                if not first:
                    act.wait_ge(s_scat[h], i * (16 * STREAMS))
                act.activation(rec_out[:, h, :, :], rec_s[:, :, bass.ds(i * 2 + h, 1), :].rearrange("p s c f -> p s (c f)"), ACT.Copy)\
                   .then_inc(s_recs[h], 1)
            for h in range(2):
                stage_records(0, h, True)
            with act.Fori(1, SBODIES) as i:
                for h in range(2):
                    stage_records(i, h, False)
            act.wait_ge(s_srt, 16)
            for l in range(LAYERS):
                with act.Fori(0, BODIES) as k:
                    for h in range(2):
                        act.wait_ge(s_prod[l][h], k + 1)
                        act.activation(idx[:, h, :], srt[:, bass.ds(k * (2 * HALF) + h * HALF, HALF), 2:3].rearrange("p c f -> p (c f)"), ACT.Copy)\
                           .then_inc(s_idx[l][h], 1)

        @block.tensor
        def _(pe):
            pe.wait_ge(s_const, 7)
            def histogram(i, h, first):
                pe.wait_ge(s_hoh[h], i + 1)
                for s in range(STREAMS):
                    last = pe.matmul(count[s], ones[:, :], onehot[:, h, s, :], start=first, stop=False, skip_group_check=True)
                last.then_inc(s_hused[h], 1)
            histogram(0, 0, True)
            histogram(0, 1, False)
            with pe.Fori(1, SBODIES) as i:
                for h in range(2):
                    histogram(i, h, False)
            pe.wait_ge(s_base, 1)
            for s in range(STREAMS):
                pe.matmul(count[s], ident[:, :], base[:, s, :], start=True, stop=False, skip_group_check=True)
            with pe.Fori(0, SBODIES) as i:
                for h in range(2):
                    pe.wait_ge(s_roh[h], i + 1)
                    for s in range(STREAMS):
                        pe.matmul(count[s], below[:, :], onehot[:, h, s, :], start=False, stop=False, skip_group_check=True)\
                          .then_inc(s_rank[h], 1)
                    for s in range(STREAMS):
                        pe.wait_ge(s_read[h], i * STREAMS + s + 1)
                        last = pe.matmul(count[s], rest[:, :], onehot[:, h, s, :], start=False, stop=False, skip_group_check=True)
                    last.then_inc(s_rused[h], 1)
            for l in range(LAYERS):
                for h in range(2):
                    pe.sem_inc(s_prod[l][h], 1)
                with pe.Fori(0, BODIES) as k:
                    for h in range(2):
                        pe.wait_ge(s_sel[l][h], k + 1)
                        pe.wait_ge(s_free[l][h], k + 1)
                        pe.wait_ge(s_got[l][h], k * (16 * HALF) + 16 * HALF)
                        for j in range(HALF):
                            last = pe.matmul(banks[h][:, j * DIM:(j + 1) * DIM], sel[:, h, j, :], got[:, h, j, :], start=True, stop=True)
                        last.then_inc(s_prod[l][h], 1)
            pe.wait_ge(s_lmw, 32)
            for c in range(KT):
                last = pe.transpose(banks[2][0:KS, c * DIM:(c + 1) * DIM], phi4_sb[:, c * KS:(c + 1) * KS], ident[0:DIM, 0:DIM])
            last.then_inc(s_lm, 1)
            pe.wait_ge(s_lmc, 1)
            for c in range(KT):
                last = pe.matmul(banks[3][0:DIM, 0:DIM], phi4T[:, c, :], ulm[:, c, :], start=(c == 0), stop=(c == KT - 1))
            last.then_inc(s_lm, 1)
            pe.wait_ge(s_lmg, 16 * 3 * GROUPS)
            pe.wait_ge(s_lmc, 3)
            for g in range(GROUPS):
                if g:
                    pe.wait_ge(s_ftc, g)
                for c in range(4):
                    pe.transpose(banks[4][0:KS, c * P:(c + 1) * P], phi2_g[:, g, c * KS:(c + 1) * KS], ident[:, :])
                for c in range(4):
                    pe.transpose(banks[5][0:KS, c * P:(c + 1) * P], phi2_g[:, g, (c + 4) * KS:(c + 5) * KS], ident[:, :])
                pe.transpose(banks[6][0:DIM, 0:P], phi3_g[:, g, :], ident[:, :]).then_inc(s_ft, 1)
                pe.wait_ge(s_ftc, g + 1)
                for c in range(KT):
                    pe.matmul(banks[7][:, g * DIM:(g + 1) * DIM], featT[0:KS, c, :], ulm9[:, c, :], start=(c == 0), stop=False, skip_group_check=True)
                pe.matmul(banks[7][:, g * DIM:(g + 1) * DIM], featT[0:DIM, KT, :], w1[:, :], start=False, stop=True, skip_group_check=True)\
                  .then_inc(s_lm, 1)

        @block.vector
        def _(dve):
            steps = [0]

            def step(ins):
                steps[0] += 1
                ins.then_inc(s_prep, 1)
                dve.wait_ge(s_prep, steps[0])

            dve.memset(raw_rows[:, FULL:COLS], BLOCKS * P).then_inc(s_tail, 1)
            dve.memset(raw_cols[:, FULL:COLS], 0).then_inc(s_tail, 1)
            dve.memset(raw_vals[:, FULL:COLS], 0.0).then_inc(s_tail, 1)
            dve.memset(srt[:, :, :], 0.0).then_inc(s_vconst, 1)
            dve.memset(zero_b[:, :], 0.0).then_inc(s_vconst, 1)
            dve.wait_ge(s_batch, 32)
            mark = sem("s_rchain")
            n = [0]

            def rstep(ins):
                n[0] += 1
                ins.then_inc(mark, 1)
                dve.wait_ge(mark, n[0])
            for side, size in ((0, N_USERS), (1, N_ITEMS)):
                rstep(dve.tensor_copy(r_f[:, side, :], r_i[:, side, :]))
                rstep(dve.tensor_scalar(r_neg[:, side, :], r_f[:, side, :], 0.0, float(size), ALU.is_lt, ALU.mult))
                rstep(dve.tensor_tensor(r_c[:, side, :], r_f[:, side, :], r_neg[:, side, :], ALU.add))
                rstep(dve.tensor_scalar(r_f[:, side, :], r_c[:, side, :], 0.0, float(size - 1), ALU.max, ALU.min))
                rstep(dve.tensor_copy(r_idx[:, side, :], r_f[:, side, :]))
                rstep(dve.tensor_scalar(n_i[:, side, :], r_f[:, side, :], float(N_USERS * side), None, ALU.add))
            rstep(dve.tensor_scalar(n_lo[:, :, :], n_i[:, :, :], P - 1, None, ALU.bitwise_and))
            rstep(dve.tensor_scalar(n_hi[:, :, :], n_i[:, :, :], 7, None, ALU.arith_shift_right))
            rstep(dve.scalar_tensor_tensor(t_idx[:, :, :], n_lo[:, :, :], float(BUCKETS), n_hi[:, :, :], ALU.mult, ALU.add))
            dve.sem_inc(s_ridx, 1)
            dve.wait_ge(s_const, 7)
            step(dve.tensor_copy(iota_b[:, :], iota_i[:, :]))
            step(dve.tensor_copy(iota_r[:, :], iota_i[:, 0:P]))
            step(dve.tensor_copy(tmap[:, :], tmap_i[:, :]))
            dve.wait_ge(s_load, 96)
            step(dve.tensor_scalar(scratch_i, raw_rows, 7, None, ALU.arith_shift_right))
            step(dve.tensor_copy(hi, scratch_i))

            def one_hots(i, h, into):
                for s in range(STREAMS):
                    last = dve.tensor_scalar(onehot[:, h, s, :], iota_b[:, :], hi[:, bass.ds(i * 2 + (h + s * SCOLS), 1)], None, ALU.is_equal)
                last.then_inc(into[h], 1)

            for h in range(2):
                one_hots(0, h, s_hoh)
            with dve.Fori(1, SBODIES) as i:
                for h in range(2):
                    dve.wait_ge(s_hused[h], i)
                    one_hots(i, h, s_hoh)
            step(dve.tensor_scalar(scratch_i, raw_rows, P - 1, None, ALU.bitwise_and))
            step(dve.tensor_copy(rec[:, :, 0], scratch_i))
            step(dve.tensor_scalar(scratch_i, raw_cols, P - 1, None, ALU.bitwise_and))
            step(dve.tensor_scalar(raw_rows, raw_cols, 7, None, ALU.arith_shift_right))
            step(dve.scalar_tensor_tensor(rec[:, :, 2], scratch_i, float(BUCKETS), raw_rows, ALU.mult, ALU.add))
            step(dve.tensor_copy(rec[:, :, 1], raw_vals))
            dve.sem_inc(s_records, 1)
            for h in range(2):
                dve.wait_ge(s_hused[h], SBODIES)
            step(dve.tensor_copy(base[:, 1, :], count[0]))
            for s in range(1, STREAMS):
                step(dve.tensor_tensor(base[:, s + 1, :], base[:, s, :], count[s], ALU.add))
            step(dve.tensor_scalar(cnt_i[:, :], base[:, STREAMS, :], float(P - 1), None, ALU.add))
            step(dve.tensor_scalar(nch_i[:, :], cnt_i[:, :], 7, None, ALU.arith_shift_right))
            step(dve.tensor_copy(nch[:, :], nch_i[:, :]))
            step(dve.tensor_tensor_scan(ends[:, :], nch[:, :], zero_b[:, :], 0.0, ALU.add, ALU.add))
            step(dve.tensor_tensor(cnt[:, :], ends[:, :], nch[:, :], ALU.subtract))
            step(dve.tensor_scalar(base[:, 0, :], cnt[:, :], float(P), None, ALU.mult))
            for s in range(1, STREAMS):
                step(dve.tensor_tensor(base[:, s, :], base[:, s, :], base[:, 0, :], ALU.add))
            dve.sem_inc(s_base, 1)
            for j in range(MAPCOLS):
                step(dve.tensor_scalar(picked[:, :], ends[:, :], tmap[:, j:j + 1], 0.0, ALU.is_le, ALU.add, accum_out=blk[:, j:j + 1]))
            step(dve.tensor_scalar(blk_i[:, :], blk[:, :], float(BUCKETS - 1), float(DIM), ALU.min, ALU.mult))
            dve.sem_inc(s_mapo, 1)

            pchain = [0]

            def places(i, h, first, nth):
                for s in range(STREAMS):
                    dve.wait_ge(s_rank[h], i * STREAMS + s + 1)
                    if s:
                        dve.wait_ge(s_read[h], i * STREAMS + s)
                    dve.scalar_tensor_tensor(picked[:, :], iota_b[:, :], hi[:, bass.ds(i * 2 + (h + s * SCOLS), 1)], count[s],
                                             ALU.is_equal, ALU.mult, accum_out=pos[:, h, s:s + 1]).then_inc(s_read[h], 1)
                dve.wait_ge(s_read[h], i * STREAMS + STREAMS)
                dve.tensor_copy(pos_i[:, h, :], pos[:, h, :]).then_inc(s_pc, 1)
                dve.wait_ge(s_pc, nth * 3 + 1)
                dve.tensor_scalar(pos_lo[:, h, :], pos_i[:, h, :], P - 1, None, ALU.bitwise_and).then_inc(s_pc, 1)
                dve.tensor_scalar(pos_hi[:, h, :], pos_i[:, h, :], 7, None, ALU.arith_shift_right).then_inc(s_pc, 1)
                dve.wait_ge(s_pc, nth * 3 + 3)
                if not first:
                    dve.wait_ge(s_scat[h], i * (16 * STREAMS))
                dve.scalar_tensor_tensor(pos_out[:, h, :], pos_lo[:, h, :], float(CHUNKS), pos_hi[:, h, :], ALU.mult, ALU.add)\
                   .then_inc(s_pos[h], 1)

            one_hots(0, 0, s_roh)
            one_hots(0, 1, s_roh)
            places(0, 0, True, 0)
            dve.wait_ge(s_rused[0], 1)
            one_hots(1, 0, s_roh)
            places(0, 1, True, 1)
            dve.wait_ge(s_rused[1], 1)
            one_hots(1, 1, s_roh)
            places(1, 0, False, 2)
            with dve.Fori(2, SBODIES) as i:
                dve.wait_ge(s_rused[0], i)
                one_hots(i, 0, s_roh)
                places(i - 1, 1, False, i * 2 - 1)
                dve.wait_ge(s_rused[1], i)
                one_hots(i, 1, s_roh)
                places(i, 0, False, i * 2)
            places(SBODIES - 1, 1, False, 2 * SBODIES - 1)

            def selectors(l, k, h):
                dve.wait_ge(s_prod[l][h], k + 1)
                for j in range(HALF):
                    c = bass.ds(k * (2 * HALF) + (h * HALF + j), 1)
                    last = dve.tensor_scalar(sel[:, h, j, :], iota_r[:, :], srt[:, c, 0], srt[:, c, 1], ALU.is_equal, ALU.mult)
                last.then_inc(s_sel[l][h], 1)

            def add_products(l, k, h):
                _, at = nc.values_load_multi_w_load_instructions(
                    chunk_map[0:1, bass.ds(k * (2 * HALF) + h * HALF, HALF)], engines=[mybir.EngineType.DVE],
                    min_val=0, max_val=(BUCKETS - 1) * DIM)
                dve.wait_ge(s_prod[l][h], k + 2)
                for j in range(HALF):
                    dst = acc[:, bass.ds(at[j], DIM)]
                    dve.wait_ge(s_add, k * (2 * HALF) + (l * CHUNKS + h * HALF + j + CREDIT))
                    last = dve.tensor_tensor(dst, dst, banks[h][:, j * DIM:(j + 1) * DIM], ALU.add).then_inc(s_add, 1)
                dve.wait_ge(s_add, k * (2 * HALF) + (l * CHUNKS + h * HALF + HALF + CREDIT))
                dve.sem_inc(s_free[l][h], 1)

            dve.wait_ge(s_srt, 16)
            dve.wait_ge(s_map, 32)
            for l in range(LAYERS):
                if l:
                    dve.wait_ge(s_tab, 16 * l)
                dve.memset(acc[:, :], 0.0).then_inc(s_zacc, 1)
                for h in range(2):
                    dve.sem_inc(s_free[l][h], 1)
                dve.wait_ge(s_zacc, l + 1)
                if l == 0:
                    dve.sem_inc(s_add, CREDIT)
                selectors(l, 0, 0)
                with dve.Fori(0, BODIES - 1) as k:
                    selectors(l, k, 1)
                    add_products(l, k, 0)
                    selectors(l, k + 1, 0)
                    add_products(l, k, 1)
                selectors(l, BODIES - 1, 1)
                add_products(l, BODIES - 1, 0)
                add_products(l, BODIES - 1, 1)

            dve.wait_ge(s_lm, 1)
            dve.tensor_copy(phi4T[:, :, :].rearrange("k c d -> k (c d)"), banks[2][0:KS, :]).then_inc(s_lmc, 1)
            dve.wait_ge(s_lm, 2)
            dve.tensor_scalar(w1[:, :], banks[3][0:DIM, 0:DIM], 0.1, None, ALU.mult).then_inc(s_lmc, 1)
            dve.tensor_scalar(ulm9[:, :, :], ulm[:, :, :], 0.9, None, ALU.mult).then_inc(s_lmc, 1)
            for g in range(GROUPS):
                if g:
                    dve.wait_ge(s_lm, 2 + g)
                dve.wait_ge(s_ft, g + 1)
                dve.tensor_copy(featT[0:KS, 0:4, :].rearrange("k c u -> k (c u)"), banks[4][0:KS, :])
                dve.tensor_copy(featT[0:KS, 4:8, :].rearrange("k c u -> k (c u)"), banks[5][0:KS, :])
                dve.tensor_copy(featT[0:DIM, KT, :], banks[6][0:DIM, 0:P]).then_inc(s_ftc, 1)
            dve.wait_ge(s_lm, 2 + GROUPS)
            dve.tensor_tensor(user_lm[:, :, :].rearrange("p g d -> p (g d)"), banks[7][:, :],
                              ilm_g[:, :, :].rearrange("p g d -> p (g d)"), ALU.mult).then_inc(s_lmc, 1)
            dve.wait_ge(s_lmc, 4)
            dve.tensor_reduce(gamma_lm[:, :], user_lm[:, :, :], AX.X, ALU.add).then_inc(s_lmc, 1)
            dve.wait_ge(s_light, 16 * 2 * GROUPS * (LAYERS + 1))
            rows_of = acc[:, 0:(LAYERS + 1) * 2 * GROUPS * DIM].rearrange("p (l n) -> p n l", l=LAYERS + 1)
            dve.tensor_reduce(light[:, :, :].rearrange("p n d -> p (n d)"), rows_of, AX.X, ALU.add).then_inc(s_lmc, 1)
            dve.wait_ge(s_lmc, 6)
            dve.tensor_tensor(user_lm[:, :, :], light[:, 0:GROUPS, :], light[:, GROUPS:2 * GROUPS, :], ALU.mult).then_inc(s_lmc, 1)
            dve.wait_ge(s_lmc, 7)
            dve.tensor_reduce(gamma_id[:, :], user_lm[:, :, :], AX.X, ALU.add).then_inc(s_lmc, 1)
            dve.wait_ge(s_lmc, 8)
            dve.scalar_tensor_tensor(result[:, :], gamma_id[:, :], 0.5 / (LAYERS + 1) ** 2, gamma_lm[:, :], ALU.mult, ALU.add)\
               .then_inc(s_fin, 1)


_INS = ['r_users', 'r_items', 'L0_rec_user_emb', 'L0_rec_item_emb', 'L0_rec_rows', 'L0_rec_cols', 'L0_rec_vals',
        'L0_rec_phi3', 'L0_rec_phi4', 'L0_rec_phi2', 'L0_rec_user_lm_T', 'L0_rec_item_lm']


def kernel(**inputs):
    import numpy as _np
    import concourse.bacc as _bacc
    from concourse import mybir as _mybir
    from concourse.bass_utils import run_bass_kernel_spmd as _run

    nc = _bacc.Bacc("TRN2", target_bir_lowering=False, num_devices=1)
    arrays, args = {}, []
    for name in _INS:
        a = _np.ascontiguousarray(inputs[name])
        arrays[f"in_{name}"] = a
        args.append(nc.dram_tensor(f"in_{name}", a.shape, _mybir.dt.from_np(a.dtype), kind="ExternalInput").ap())
    batch = arrays["in_r_users"].shape[0]
    out = nc.dram_tensor("out_scores", (batch,), _mybir.dt.float32, kind="ExternalOutput").ap()
    rec_kernel(nc, *args, out)
    r = _run(nc, [arrays], core_ids=[0])
    return r.results[0]["out_scores"]
```

```python
import numpy as np
import concourse.bass as bass
from concourse import mybir
from contextlib import ExitStack

"""LightGCN propagation (three sparse matrix products) and batch scores.

The edges are sorted on the chip by the 128-node block of their row (a counting sort: a histogram, then
each edge's rank by one-hot matrix products, then an indirect scatter).  A layer then walks the sorted
edges in chunks of 128 that all lie in one block: GpSimd gathers the chunk's source rows, TensorE
multiplies them with a [edge, row-in-block] matrix that holds the edge's value (its product sums the edges
of each row), and VectorE adds the product to the block's accumulator in SBUF.

Node n is at partition n % 128, block n // 128 on chip, and at row (n % 128) * BUCKETS + n // 128 of the
embedding tables in DRAM, so that the accumulators go out in one contiguous run per partition.
"""


def rec_kernel(nc, r_users, r_items, user_emb, item_emb, rows, cols, vals, phi3, phi4, phi2, user_lm_T,
               item_lm, out):
    f32, f16, i32, i16 = mybir.dt.float32, mybir.dt.float16, mybir.dt.int32, mybir.dt.int16
    ALU = mybir.AluOpType
    ACT = mybir.ActivationFunctionType
    AX = mybir.AxisListType

    P = 128
    N_USERS, DIM = user_emb.shape
    N_ITEMS = item_emb.shape[0]
    N_NODES = N_USERS + N_ITEMS
    NNZ = rows.shape[0]
    BATCH = r_users.shape[0]
    M_PHI = phi2.shape[1]
    LAYERS = 3

    BLOCKS = -(-N_NODES // P)
    BUCKETS = BLOCKS + 1
    STREAMS = 5
    FULL = NNZ // P
    TAIL = NNZ - FULL * P
    HC = 16
    HA = -(-BUCKETS // HC)
    HG = P // HA
    SCOLS = -(-(FULL + 1) // (2 * HG * STREAMS)) * 2 * HG
    HM = next(m for m in range(8, 0, -1) if SCOLS // HG % m == 0)
    HCOLS = HM * HG
    HSTEPS = SCOLS // HCOLS
    COLS = SCOLS * STREAMS
    SBODIES = SCOLS // 2
    HALF = 8
    SETS = -(-((COLS * P + BUCKETS * P) // P) // (4 * HALF)) * 2
    CHUNKS = SETS * 2 * HALF
    LOOK_BODIES = SETS // 2
    BODIES = CHUNKS // (2 * HALF)
    MAPCOLS = -(-CHUNKS // P)
    GROUPS = BATCH // P
    SLOTS = 2 * GROUPS
    KT = 8
    CREDIT = 1
    KS = M_PHI // KT

    tables = [nc.dram_tensor(f"table{l}", (P * BUCKETS, DIM), f32, kind="Internal").ap() for l in range(LAYERS)]
    sorted_dram = nc.dram_tensor("sorted_edges", (P * CHUNKS, 3), f32, kind="Internal").ap()
    first_dram = nc.dram_tensor("chunk_first_node", (MAPCOLS * P,), f16, kind="Internal").ap()
    nodes_dram = nc.dram_tensor("batch_nodes", (P * SLOTS,), f32, kind="Internal").ap()

    ctx = ExitStack()
    with ctx:
        def sb(name, shape, dt=f32):
            return ctx.enter_context(nc.sbuf_tensor(name, shape, dt))

        def pb(name, shape, dt=f32):
            return ctx.enter_context(nc.psum_tensor(name, shape, dt))

        def sem(name):
            return ctx.enter_context(nc.semaphore(name))

        acc = sb("acc", [P, (BUCKETS + HALF - 1) * DIM])
        raw_rows = acc[:, 0:COLS].bitcast(i32)
        raw_cols = acc[:, COLS:2 * COLS].bitcast(i32)
        raw_vals = acc[:, 2 * COLS:3 * COLS]
        scratch_i = acc[:, 3 * COLS:4 * COLS].bitcast(i32)
        hi = acc[:, 4 * COLS:5 * COLS]
        hi_a = acc[:, 5 * COLS:5 * COLS + COLS // 2].bitcast(f16)
        hi_c = acc[:, 5 * COLS + COLS // 2:6 * COLS].bitcast(f16)
        rec = sb("rec", [P, COLS, 3])
        rec_s = rec[:, :, :].rearrange("p (s c) f -> p s c f", s=STREAMS)
        srt = sb("srt", [P, CHUNKS, 3])
        phi2_g = srt[:, :, :].rearrange("p c f -> p (c f)")[:, 0:GROUPS * M_PHI].rearrange("p (g m) -> p g m", g=GROUPS)

        def carver(flat):
            at = [0]

            def carve(shape, dt=f32):
                width = int(np.prod(shape[1:]))
                words = width if dt in (f32, i32) else -(-width // 2)
                part = flat[0:shape[0], at[0]:at[0] + words]
                at[0] += words
                assert at[0] <= flat.shape[1]
                if dt != f32:
                    part = part.bitcast(dt)
                if len(shape) == 2:
                    return part
                names = "abc"[:len(shape) - 1]
                return part.rearrange(f"p ({' '.join(names)}) -> p {' '.join(names)}", **dict(zip(names, shape[1:])))
            return carve

        after_sort = carver(rec[:, :, :].rearrange("p c f -> p (c f)"))
        after_layers = carver(acc[:, :])
        room = sb("room", [P, 5 * P * HALF + 256])
        for_sort = carver(room[:, :])
        for_layers = carver(room[:, :])

        KB = 3
        BP = BUCKETS // KB
        TS = 8
        TW = CHUNKS // TS
        for_hist = carver(room[:, :])
        is_a = for_hist([P, STREAMS, HCOLS, HA], f16)
        is_c = for_hist([P, STREAMS, HCOLS, HC], f16)
        folded = for_hist([P, STREAMS, HG, HC])
        part_of = for_hist([P, STREAMS, HC])
        spread_c = for_hist([P, 2, HA, HC])
        own_group = for_hist([P, HG, HC])
        own_as = for_hist([P, HA, HG])
        own_a = for_hist([P, HA])
        iota_i = sb("iota_i", [P, BUCKETS], i32)
        iota_b = sb("iota_b", [P, BUCKETS], f16)
        iota_r = sb("iota_r", [P, P])
        tmap_i = sb("tmap_i", [P, MAPCOLS], i32)
        tmap = sb("tmap", [P, MAPCOLS])
        ident = sb("ident", [P, P])
        assert CHUNKS % 8 == 0 and BUCKETS % 3 == 0
        ident_h = sb("ident_h", [P, P], f16)
        ones = sb("ones", [P, P], f16)
        below = sb("below", [P, P], f16)
        rest = sb("rest", [P, P], f16)
        onehot = for_sort([P, 2, STREAMS, BUCKETS], f16)
        picked = for_sort([P, BUCKETS])
        pos = sb("pos", [P, 2, STREAMS])
        pos_i = sb("pos_i", [P, 2, STREAMS], i32)
        pos_lo = sb("pos_lo", [P, 2, STREAMS], i32)
        pos_hi = sb("pos_hi", [P, 2, STREAMS], i32)
        pos_out = sb("pos_out", [P, 2, STREAMS], i32)
        rec_out = sb("rec_out", [P, 2, STREAMS, 3])
        bucket_is = onehot[:, :, :, :].rearrange("p a s b -> p (a s b)")[:, 0:2 * KB * TW].rearrange("p (a c t) -> p a c t", a=2, c=KB)
        base = for_sort([P, STREAMS + 1, BUCKETS])
        cnt = for_sort([P, BUCKETS])
        cnt_i = for_sort([P, BUCKETS], i32)
        nch_i = for_sort([P, BUCKETS], i32)
        nch = for_sort([P, BUCKETS])
        ends = for_sort([P, BUCKETS])
        zero_b = sb("zero_b", [P, BUCKETS])
        blk = sb("blk", [P, MAPCOLS])
        first_16 = sb("first_16", [P, MAPCOLS], f16)
        ahead = sb("ahead", [1, CHUNKS], i16)
        first_d = acc[:, 0:CHUNKS]
        window = sb("window", [1, CHUNKS // HALF], i32)
        first = sb("first", [P, CHUNKS], f16)
        ones_f = sb("ones_f", [P, P])
        zero_h = sb("zero_h", [P, P], f16)
        zero_w = sb("zero_w", [P, HALF * DIM], f16)
        val = sb("val", [P, 2, HALF])
        part_node_i = sb("part_node_i", [P, KB], i32)
        part_node = sb("part_node", [P, KB])
        wantedT = sb("wantedT", [BP, KB, P], f16)
        wanted_at = sb("wanted_at", [P, CHUNKS], f16)
        low = sb("low", [P, 2, HALF])
        flags = sb("flags", [P, CHUNKS], f16)
        wanted = sb("wanted", [P, BUCKETS], f16)
        wanted_8 = sb("wanted_8", [P, 2, HALF], f16)
        look_low = sb("look_low", [P, 2, HALF])
        look = for_layers([P, 2, HALF, P], f16)
        lookT = for_layers([P, 2, HALF, P], f16)
        row_base = sb("row_base", [P, 1])
        row_base_i = sb("row_base_i", [P, 1], i32)
        keys = after_layers([P, CHUNKS])
        top = after_layers([P, 8])
        valid = after_layers([P, 2, 8])
        at_f = after_layers([P, 8])
        at_i = after_layers([P, 8], i32)
        src_i = after_layers([P, 2, 8], i32)
        val8 = after_layers([P, 2, 8])
        found = after_layers([P, 2, 8, 3])
        source = after_layers([P, 2, 8, DIM])
        nodes_in = after_layers([P, P * SLOTS])
        nodes = after_layers([P, SLOTS, P])
        match = after_layers([P, 2, SLOTS * P])
        zero_t = after_layers([P, 512])
        near = after_layers([P, 1])
        rounds_f = after_layers([1, 4])
        rounds_i = after_layers([1, 2], i32)
        tabs_g = after_layers([P, LAYERS, SLOTS, DIM])
        idx = sb("idx", [P, 2, HALF], i32)
        got = for_layers([P, 2, HALF, DIM])
        sel = for_layers([P, 2, HALF, P])

        r_i = sb("r_i", [P, 2, GROUPS], i32)
        r_f = sb("r_f", [P, 2, GROUPS])
        r_neg = sb("r_neg", [P, 2, GROUPS])
        r_c = sb("r_c", [P, 2, GROUPS])
        r_idx = sb("r_idx", [P, 2, GROUPS], i32)
        n_f = sb("n_f", [P, 2, GROUPS])
        n_lo_f = sb("n_lo_f", [P, 2, GROUPS])
        n_hi_f = sb("n_hi_f", [P, 2, GROUPS])
        mark_lo = sb("mark_lo", [P, 2, P], f16)
        n_i = sb("n_i", [P, 2, GROUPS], i32)
        n_lo = sb("n_lo", [P, 2, GROUPS], i32)
        n_hi = sb("n_hi", [P, 2, GROUPS], i32)
        t_idx = sb("t_idx", [P, 2, GROUPS], i32)
        phi3_g = after_sort([P, GROUPS, DIM])
        ilm_g = after_sort([P, GROUPS, DIM])
        phi4_sb = after_sort([DIM, M_PHI])
        ulm = after_sort([KS, KT, DIM])
        phi4T = after_sort([KS, KT, DIM])
        w1 = after_sort([DIM, DIM])
        ulm9 = after_sort([KS, KT, DIM])
        featT = after_sort([P, KT + 1, P])
        user_lm = after_sort([P, GROUPS, DIM])
        gamma_lm = sb("gamma_lm", [P, GROUPS])
        gamma_id = sb("gamma_id", [P, GROUPS])
        result = sb("result", [P, GROUPS])
        light = after_layers([P, 2 * GROUPS, DIM])
    
        banks = [pb(f"bank{i}", [P, 512]) for i in range(8)]
        count = [banks[s][:, 0:BUCKETS] for s in range(STREAMS)]

        s_load = sem("s_load")
        s_tab0 = sem("s_tab0")
        s_batch = sem("s_batch")
        s_lmw = sem("s_lmw")
        s_const = sem("s_const")
        s_vconst = sem("s_vconst")
        s_tail = sem("s_tail")
        s_prep = sem("s_prep")
        s_records = sem("s_records")
        s_ridx = sem("s_ridx")
        s_lmg = sem("s_lmg")
        s_hoh = [sem(f"s_hoh{st}") for st in range(STREAMS)]
        s_hused = [sem(f"s_hused{st}") for st in range(STREAMS)]
        s_hfold = sem("s_hfold")
        s_hspread = sem("s_hspread")
        s_counted = sem("s_counted")
        s_ones = sem("s_ones")
        s_zsrt = sem("s_zsrt")
        s_base = sem("s_base")
        s_roh = [sem(f"s_roh{h}") for h in range(2)]
        s_rank = [sem(f"s_rank{h}") for h in range(2)]
        s_read = [sem(f"s_read{h}") for h in range(2)]
        s_rused = [sem(f"s_rused{h}") for h in range(2)]
        s_recs = [sem(f"s_recs{h}") for h in range(2)]
        s_pos = [sem(f"s_pos{h}") for h in range(2)]
        s_pc = sem("s_pc")
        s_scat = [sem(f"s_scat{h}") for h in range(2)]
        s_mapo = sem("s_mapo")
        s_map = sem("s_map")
        s_srt = sem("s_srt")
        s_idx = [[sem(f"s_idx{l}{h}") for h in range(2)] for l in range(LAYERS - 1)]
        s_val = [[sem(f"s_val{l}{h}") for h in range(2)] for l in range(LAYERS - 1)]
        s_got = [[sem(f"s_got{l}{h}") for h in range(2)] for l in range(LAYERS - 1)]
        s_sel = [[sem(f"s_sel{l}{h}") for h in range(2)] for l in range(LAYERS - 1)]
        s_prod = [[sem(f"s_prod{l}{h}") for h in range(2)] for l in range(LAYERS - 1)]
        s_free = [[sem(f"s_free{l}{h}") for h in range(2)] for l in range(LAYERS - 1)]
        s_nodes = sem("s_nodes")
        s_nf = sem("s_nf")
        s_mark = sem("s_mark")
        s_marked = sem("s_marked")
        s_wanted = sem("s_wanted")
        s_look = [sem(f"s_look{h}") for h in range(2)]
        s_turned = [sem(f"s_turned{h}") for h in range(2)]
        s_lookT = [sem(f"s_lookT{h}") for h in range(2)]
        s_asked = [sem(f"s_asked{h}") for h in range(2)]
        s_flag = [sem(f"s_flag{h}") for h in range(2)]
        s_low = sem("s_low")
        s_windows = sem("s_windows")
        s_expand = sem("s_expand")
        s_expanded = sem("s_expanded")
        s_wT = sem("s_wT")
        s_wTc = sem("s_wTc")
        s_wat = sem("s_wat")
        s_llow = sem("s_llow")
        s_fold = sem("s_fold")
        s_win = sem("s_win")
        s_near = sem("s_near")
        s_nearT = sem("s_nearT")
        s_rounds = sem("s_rounds")
        s_top = sem("s_top")
        s_at = sem("s_at")
        s_found = sem("s_found")
        s_src = sem("s_src")
        s_source = [sem(f"s_source{b}") for b in range(2)]
        s_match = [sem(f"s_match{h}") for h in range(2)]
        s_matched = [sem(f"s_matched{h}") for h in range(2)]
        s_zacc = sem("s_zacc")
        s_add = sem("s_add")
        s_tab = sem("s_tab")
        s_fin = sem("s_fin")
        s_light = sem("s_light")
        s_ft = sem("s_ft")
        s_ftc = sem("s_ftc")
        s_lm = sem("s_lm")
        s_lmc = sem("s_lmc")
        s_out = sem("s_out")

        block = ctx.enter_context(nc.Block())
        U0 = N_USERS // P
        UR = N_USERS - U0 * P
        I0 = P - UR
        IB = (N_ITEMS - I0) // P
        IR = N_ITEMS - I0 - IB * P

        @block.sync
        def _(sp):
            sp.wait_ge(s_tail, 3)
            for raw, dram in ((raw_rows, rows), (raw_cols, cols), (raw_vals, vals)):
                sp.dma_start(raw[:, 0:FULL], dram[0:FULL * P].rearrange("(p n) -> p n", p=P)).then_inc(s_load, 16)
                sp.dma_start(raw[0:TAIL, FULL:FULL + 1], dram[FULL * P:NNZ].rearrange("(p n) -> p n", n=1)).then_inc(s_load, 16)
            sp.dma_start(r_i[:, 0, :], r_users.rearrange("(p g) -> p g", g=GROUPS)).then_inc(s_batch, 16)
            sp.dma_start(r_i[:, 1, :], r_items.rearrange("(p g) -> p g", g=GROUPS)).then_inc(s_batch, 16)
            sp.wait_ge(s_nf, 1)
            sp.dma_start(nodes_dram.rearrange("(p q) -> p q", p=P), n_f[:, :, :].rearrange("p s g -> p (s g)")).then_inc(s_nodes, 16)
            sp.wait_ge(s_vconst, 1)
            sp.dma_start(sorted_dram.rearrange("(p c) f -> p (c f)", p=P),
                         srt[:, :, :].rearrange("p c f -> p (c f)")).then_inc(s_zsrt, 16)
            t0 = tables[0].rearrange("(p b) d -> p b d", p=P)
            sp.dma_start(t0[:, 0:U0, :], user_emb[0:U0 * P, :].rearrange("(b p) d -> p b d", p=P)).then_inc(s_tab0, 16)
            sp.dma_start(t0[0:UR, U0, :], user_emb[U0 * P:N_USERS, :]).then_inc(s_tab0, 16)
            sp.dma_start(t0[UR:P, U0, :], item_emb[0:I0, :]).then_inc(s_tab0, 16)
            sp.dma_start(t0[:, U0 + 1:U0 + 1 + IB, :], item_emb[I0:I0 + IB * P, :].rearrange("(b p) d -> p b d", p=P)).then_inc(s_tab0, 16)
            sp.dma_start(t0[0:IR, U0 + 1 + IB, :], item_emb[I0 + IB * P:N_ITEMS, :]).then_inc(s_tab0, 16)
            zeros = srt[:, :, :].rearrange("p c f -> p (c f)")[:, 0:DIM]
            sp.dma_start(t0[IR:P, U0 + 1 + IB, :], zeros[IR:P, :]).then_inc(s_tab0, 16)
            sp.dma_start(t0[:, BLOCKS, :], zeros).then_inc(s_tab0, 16)
            sp.wait_ge(s_mapo, 1)
            sp.dma_start(first_dram.rearrange("(p j) -> p j", p=P), first_16[:, :]).then_inc(s_map, 16)
            sp.wait_ge(s_map, 16)
            sp.dma_start(first[:, :], first_dram[0:CHUNKS].partition_broadcast(P)).then_inc(s_map, 16)
            for h in range(2):
                sp.wait_ge(s_scat[h], 16 * STREAMS * SBODIES)
            sp.wait_ge(s_tab0, 112)
            sp.dma_start(srt[:, :, :].rearrange("p c f -> p (c f)"),
                         sorted_dram.rearrange("(p c) f -> p (c f)", p=P)).then_inc(s_srt, 16)
            for l in range(LAYERS - 1):
                sp.wait_ge(s_add, CREDIT + 2 * BODIES * (l + 1))
                sp.dma_start(tables[l + 1].rearrange("(p b) d -> p (b d)", p=P), acc[:, 0:BUCKETS * DIM]).then_inc(s_tab, 16)
            sp.dma_start(phi4_sb, phi4).then_inc(s_lmw, 16)
            sp.dma_start(ulm, user_lm_T.rearrange("(c k) d -> k c d", k=KS)).then_inc(s_lmw, 16)
            sp.wait_ge(s_tab, 16 * (LAYERS - 1))
            sp.wait_ge(s_nodes, 16)
            sp.dma_start(nodes_in, nodes_dram.partition_broadcast(P)).then_inc(s_nodes, 16)
            sp.wait_ge(s_fin, 1)
            sp.dma_start(out.rearrange("(p g) -> p g", g=GROUPS), result[:, :]).then_inc(s_out, 16)
            sp.wait_ge(s_out, 16)

        @block.gpsimd
        def _(pool):
            pool.iota(iota_i[:, :], pattern=[[1, BUCKETS]], base=0, channel_multiplier=0).then_inc(s_const, 1)
            pool.iota(tmap_i[:, :], pattern=[[1, MAPCOLS]], base=0, channel_multiplier=MAPCOLS).then_inc(s_const, 1)
            pool.memset(ones[:, :], 1.0).then_inc(s_const, 1)
            pool.memset(ident[:, :], 0.0).then_inc(s_const, 1)
            pool.iota(row_base_i[:, :], pattern=[[0, 1]], base=0, channel_multiplier=CHUNKS).then_inc(s_const, 1)
            pool.iota(part_node_i[:, :], pattern=[[P * BP, KB]], base=0, channel_multiplier=P).then_inc(s_const, 1)
            pool.memset(zero_h[:, :], 0.0).then_inc(s_const, 1)
            pool.memset(zero_w[:, :], 0.0).then_inc(s_const, 1)
            pool.memset(own_group[:, :, :], 1.0).then_inc(s_const, 1)
            pool.memset(own_as[:, :, :], 0.0).then_inc(s_const, 1)
            pool.wait_ge(s_const, 10)
            pool.affine_select(out=own_group[:, :, :], in_=own_group[:, :, :], compare_op=ALU.is_ge, fill=0.0,
                               base=0, pattern=[[-HA, HG], [0, HC]], channel_multiplier=1).then_inc(s_const, 1)
            pool.affine_select(out=own_as[:, :, :], in_=own_as[:, :, :], compare_op=ALU.not_equal, fill=1.0,
                               base=0, pattern=[[-1, HA], [-HA, HG]], channel_multiplier=1).then_inc(s_const, 1)
            pool.wait_ge(s_const, 12)
            pool.affine_select(out=own_group[:, :, :], in_=own_group[:, :, :], compare_op=ALU.is_ge, fill=0.0,
                               base=HA - 1, pattern=[[HA, HG], [0, HC]], channel_multiplier=-1).then_inc(s_const, 1)
            pool.affine_select(out=ident[:, :], in_=ident[:, :], compare_op=ALU.not_equal, fill=1.0,
                               base=0, pattern=[[-1, P]], channel_multiplier=1).then_inc(s_const, 1)
            pool.affine_select(out=below[:, :], in_=ones[:, :], compare_op=ALU.is_gt, fill=0.0,
                               base=0, pattern=[[1, P]], channel_multiplier=-1).then_inc(s_const, 1)
            pool.affine_select(out=rest[:, :], in_=ones[:, :], compare_op=ALU.is_ge, fill=0.0,
                               base=0, pattern=[[-1, P]], channel_multiplier=1).then_inc(s_const, 1)
            pool.wait_ge(s_zsrt, 16)
            with pool.Fori(0, SBODIES) as i:
                for h in range(2):
                    pool.wait_ge(s_recs[h], i + 1)
                    pool.wait_ge(s_pos[h], i + 1)
                    pool.nop(nofuse=True)
                    for s in range(STREAMS):
                        pool.indirect_dma_start(sorted_dram, bass.IndirectOffsetOnAxis(pos_out[:, h, s:s + 1], 0),
                                                rec_out[:, h, s, :], None).then_inc(s_scat[h], 16)
            pool.wait_ge(s_tab0, 112)
            for l in range(LAYERS - 1):
                if l:
                    pool.wait_ge(s_tab, 16 * l)
                with pool.Fori(0, BODIES) as k:
                    for h in range(2):
                        pool.wait_ge(s_idx[l][h], k + 1)
                        pool.nop(nofuse=True)
                        for j in range(HALF):
                            pool.indirect_dma_start(got[:, h, j, :], None, tables[l],
                                                    bass.IndirectOffsetOnAxis(idx[:, h, j:j + 1], 0))\
                                .then_inc(s_got[l][h], 16)
            pool.wait_ge(s_add, CREDIT + 2 * BODIES * (LAYERS - 1))
            for g in range(GROUPS):
                for dst, src, side in ((phi2_g, phi2, 0), (phi3_g, phi3, 0), (ilm_g, item_lm, 1)):
                    pool.indirect_dma_start(dst[:, g, :], None, src, bass.IndirectOffsetOnAxis(r_idx[:, side, g:g + 1], 0))\
                        .then_inc(s_lmg, 16)
            pool.wait_ge(s_tab, 16 * (LAYERS - 1))
            for l in range(LAYERS):
                for side in range(2):
                    for g in range(GROUPS):
                        pool.indirect_dma_start(tabs_g[:, l, side * GROUPS + g, :], None, tables[l],
                                                bass.IndirectOffsetOnAxis(t_idx[:, side, g:g + 1], 0)).then_inc(s_light, 16)
            pool.wait_ge(s_rounds, 1)
            turns = pool.value_load(rounds_i[0:1, 0:1], min_val=1, max_val=CHUNKS // 8)

            def find(r, b):
                pool.wait_ge(s_at, r + 1)
                pool.nop(nofuse=True)
                for j in range(8):
                    pool.indirect_dma_start(found[:, b, j, :], None, sorted_dram,
                                            bass.IndirectOffsetOnAxis(at_i[:, j:j + 1], 0)).then_inc(s_found, 16)
                pool.wait_ge(s_src, r + 1)
                pool.nop(nofuse=True)
                for j in range(8):
                    pool.indirect_dma_start(source[:, b, j, :], None, tables[LAYERS - 1],
                                            bass.IndirectOffsetOnAxis(src_i[:, b, j:j + 1], 0)).then_inc(s_source[b], 16)
            with pool.Fori(0, turns) as r:
                for b in range(2):
                    find(r * 2 + b, b)

        @block.scalar
        def _(act):
            act.wait_ge(s_records, 1)

            def stage_records(i, h, first):
                if not first:
                    act.wait_ge(s_scat[h], i * (16 * STREAMS))
                act.activation(rec_out[:, h, :, :], rec_s[:, :, bass.ds(i * 2 + h, 1), :].rearrange("p s c f -> p s (c f)"), ACT.Copy)\
                   .then_inc(s_recs[h], 1)
            for h in range(2):
                stage_records(0, h, True)
            with act.Fori(1, SBODIES) as i:
                for h in range(2):
                    stage_records(i, h, False)
            act.wait_ge(s_srt, 16)
            def stage_indices(l, k, h):
                act.wait_ge(s_prod[l][h], k + 1)
                here = bass.ds(k * (2 * HALF) + h * HALF, HALF)
                act.activation(idx[:, h, :], srt[:, here, 2], ACT.Copy).then_inc(s_idx[l][h], 1)
                act.activation(val[:, h, :], srt[:, here, 1], ACT.Copy).then_inc(s_val[l][h], 1)

            def turned(q):
                for b in range(2):
                    act.wait_ge(s_turned[b], q + 2)
                    act.activation(wanted_8[:, b, :], wanted_at[:, bass.ds(q * (2 * HALF) + b * HALF, HALF)], ACT.Copy)
                    act.activation(lookT[:, b, :, :].rearrange("p j e -> p (j e)"), banks[2 + b][:, :].bitcast(f16), ACT.Copy)\
                       .then_inc(s_lookT[b], 1)

            def flagged(q):
                for b in range(2):
                    act.wait_ge(s_asked[b], q + 1)
                    act.activation(flags[:, bass.ds(q * (2 * HALF) + b * HALF, HALF)], banks[4 + b][:, 0:HALF], ACT.Copy)\
                       .then_inc(s_flag[b], 1)

            act.wait_ge(s_wT, 1)
            act.activation(wantedT[:, :, :].rearrange("b c r -> b (c r)"), banks[7][0:BP, :].bitcast(f16)[:, 0:KB * P], ACT.Copy).then_inc(s_wTc, 1)
            for n in range(TS):
                act.wait_ge(s_expanded, n + 1)
                act.activation(wanted_at[:, n * TW:(n + 1) * TW], banks[5 + n % 2][:, 0:TW], ACT.Copy).then_inc(s_wat, 1)
            for l in range(LAYERS - 1):
                stage_indices(l, 0, 0)
                stage_indices(l, 0, 1)
                if l == 0:
                    stage_indices(l, 1, 0)
                    turned(0)
                    stage_indices(l, 1, 1)
                    flagged(0)
                    turned(1)
                    with act.Fori(1, LOOK_BODIES) as k:
                        for h in range(2):
                            stage_indices(l, k + 1, h)
                            flagged(k * 2 + (h - 1))
                            turned(k * 2 + h)
                    flagged(SETS - 1)
                with act.Fori(LOOK_BODIES if l == 0 else 0, BODIES - 1) as k:
                    for h in range(2):
                        stage_indices(l, k + 1, h)

        @block.tensor
        def _(pe):
            pe.wait_ge(s_const, 16)
            for q in range(SLOTS):
                pe.wait_ge(s_mark, q + 1)
                pe.matmul(banks[5][:, 0:BUCKETS], mark_lo[:, q % 2, :], onehot[:, 0, q % 2, :], start=(q == 0), stop=(q == SLOTS - 1))\
                  .then_inc(s_marked, 1)
            HR = HG * HA
            for st in range(STREAMS):
                pe.matmul(banks[st][0:HR, 0:HG * HC], zero_h[:, 0:HR], zero_w[:, 0:HG * HC], start=True, stop=False, skip_group_check=True)
            with pe.Fori(0, HSTEPS) as i:
                for st in range(STREAMS):
                    pe.wait_ge(s_hoh[st], i + 1)
                    for m in range(HM):
                        part = slice(m * HG, (m + 1) * HG)
                        last = pe.matmul(banks[st][0:HR, 0:HG * HC], is_a[:, st, part, :].rearrange("p g a -> p (g a)"),
                                         is_c[:, st, part, :].rearrange("p g c -> p (g c)"), start=False, stop=False, skip_group_check=True)
                    last.then_inc(s_hused[st], 1)
            pe.wait_ge(s_ones, 1)
            for st in range(STREAMS):
                pe.wait_ge(s_hspread, st + 1)
                pe.matmul(banks[st][:, 0:HA * HC], ones_f[0:HR, :], spread_c[0:HR, st % 2, :, :].rearrange("p a c -> p (a c)"), start=True, stop=True)\
                  .then_inc(s_counted, 1)
            pe.wait_ge(s_base, 1)
            for s in range(STREAMS):
                pe.matmul(count[s], ident[:, :], base[:, s, :], start=True, stop=False, skip_group_check=True)
            with pe.Fori(0, SBODIES) as i:
                for h in range(2):
                    pe.wait_ge(s_roh[h], i + 1)
                    for s in range(STREAMS):
                        pe.matmul(count[s], below[:, :], onehot[:, h, s, :], start=False, stop=False, skip_group_check=True)\
                          .then_inc(s_rank[h], 1)
                    for s in range(STREAMS):
                        pe.wait_ge(s_read[h], i * STREAMS + s + 1)
                        last = pe.matmul(count[s], rest[:, :], onehot[:, h, s, :], start=False, stop=False, skip_group_check=True)
                    last.then_inc(s_rused[h], 1)
            zeros_h = zero_w[:, :]

            def products(l, k, h):
                _, at = nc.values_load_multi_w_load_instructions(
                    ahead[0:1, bass.ds(k * (2 * HALF) + h * HALF, HALF)],
                    engines=[mybir.EngineType.PE], min_val=0, max_val=(HALF - 1) * DIM)
                pe.wait_ge(s_sel[l][h], k + 1)
                pe.wait_ge(s_free[l][h], k + 1)
                pe.wait_ge(s_got[l][h], k * (16 * HALF) + 16 * HALF)
                pe.matmul(banks[h][:, :], zero_h[:, :], zeros_h, start=True, stop=False, skip_group_check=True)
                for j in range(HALF):
                    last = pe.matmul(banks[h][:, bass.ds(at[j], DIM)], sel[:, h, j, :], got[:, h, j, :], start=False, stop=(j == HALF - 1), skip_group_check=True)
                last.then_inc(s_prod[l][h], 1)

            def turn_over(q):
                for b in range(2):
                    pe.wait_ge(s_look[b], q + 1)
                    for j in range(HALF):
                        last = pe.transpose(banks[2 + b][:, :].bitcast(f16)[:, j * P:(j + 1) * P], look[:, b, j, :], ident_h[:, :])
                    last.then_inc(s_turned[b], 1)

            def ask(q):
                for b in range(2):
                    pe.wait_ge(s_lookT[b], q + 1)
                    pe.wait_ge(s_flag[b], q + 1)
                    for j in range(HALF):
                        last = pe.matmul(banks[4 + b][:, j:j + 1], lookT[:, b, j, :], wanted_8[:, b, j:j + 1], start=True, stop=True)
                    last.then_inc(s_asked[b], 1)

            pe.wait_ge(s_wanted, 1)
            for c in range(KB):
                last = pe.transpose(banks[7][0:BP, :].bitcast(f16)[:, c * P:(c + 1) * P], wanted[:, c * BP:(c + 1) * BP], ident_h[:, :])
            last.then_inc(s_wT, 1)
            pe.wait_ge(s_wTc, 1)
            for n in range(TS):
                pe.wait_ge(s_expand, n + 1)
                if n >= 2:
                    pe.wait_ge(s_wat, n - 1)
                for c in range(KB):
                    last = pe.matmul(banks[5 + n % 2][:, 0:TW], wantedT[:, c, :], bucket_is[0:BP, n % 2, c, :], start=(c == 0), stop=(c == KB - 1))
                last.then_inc(s_expanded, 1)
            pe.wait_ge(s_wat, TS)
            pe.wait_ge(s_windows, 1)
            for l in range(LAYERS - 1):
                for h in range(2):
                    pe.sem_inc(s_prod[l][h], 1)
                if l == 0:
                    for b in range(2):
                        pe.sem_inc(s_turned[b], 1)
                        pe.sem_inc(s_flag[b], 1)
                    products(l, 0, 0)
                    turn_over(0)
                    products(l, 0, 1)
                    ask(0)
                    turn_over(1)
                    with pe.Fori(1, LOOK_BODIES) as k:
                        for h in range(2):
                            products(l, k, h)
                            ask(k * 2 + (h - 1))
                            turn_over(k * 2 + h)
                    ask(SETS - 1)
                with pe.Fori(LOOK_BODIES if l == 0 else 0, BODIES) as k:
                    for h in range(2):
                        products(l, k, h)
            pe.wait_ge(s_near, 2)
            pe.transpose(banks[4][0:1, 0:P], near, ident[:, :]).then_inc(s_nearT, 1)
            pe.wait_ge(s_rounds, 1)
            turns = pe.value_load(rounds_i[0:1, 0:1], min_val=1, max_val=CHUNKS // 8)
            for b in range(2):
                pe.matmul(banks[6 + b][:, :], zero_t[:, 0:P], zero_t[:, :], start=True, stop=False, skip_group_check=True)

            for i in range(2):
                pe.sem_inc(s_matched[i], 1)

            def spread(r, b):
                pe.wait_ge(s_source[b], r * (16 * 8) + 16 * 8)
                for j in range(8):
                    pe.wait_ge(s_match[j % 2], r * 8 + (b * 4 + j // 2 + 1))
                    for q in range(SLOTS):
                        last = pe.matmul(banks[6 + q // GROUPS][:, (q % GROUPS) * DIM:(q % GROUPS + 1) * DIM],
                                         match[:, j % 2, q * P:(q + 1) * P], source[:, b, j, :], start=False, stop=False, skip_group_check=True)
                    last.then_inc(s_matched[j % 2], 1)
            with pe.Fori(0, turns) as r:
                for b in range(2):
                    spread(r, b)
            pe.wait_ge(s_lmw, 32)
            for c in range(KT):
                last = pe.transpose(banks[2][0:KS, c * DIM:(c + 1) * DIM], phi4_sb[:, c * KS:(c + 1) * KS], ident[0:DIM, 0:DIM])
            last.then_inc(s_lm, 1)
            pe.wait_ge(s_lmc, 1)
            for c in range(KT):
                last = pe.matmul(banks[3][0:DIM, 0:DIM], phi4T[:, c, :], ulm[:, c, :], start=(c == 0), stop=(c == KT - 1))
            last.then_inc(s_lm, 1)
            pe.wait_ge(s_lmg, 16 * 3 * GROUPS)
            pe.wait_ge(s_lmc, 3)
            for g in range(GROUPS):
                if g:
                    pe.wait_ge(s_ftc, g)
                for c in range(4):
                    pe.transpose(banks[4][0:KS, c * P:(c + 1) * P], phi2_g[:, g, c * KS:(c + 1) * KS], ident[:, :])
                for c in range(4):
                    pe.transpose(banks[5][0:KS, c * P:(c + 1) * P], phi2_g[:, g, (c + 4) * KS:(c + 5) * KS], ident[:, :])
                pe.transpose(banks[1][0:DIM, 0:P], phi3_g[:, g, :], ident[:, :]).then_inc(s_ft, 1)
                pe.wait_ge(s_ftc, g + 1)
                for c in range(KT):
                    pe.matmul(banks[0][:, g * DIM:(g + 1) * DIM], featT[0:KS, c, :], ulm9[:, c, :], start=(c == 0), stop=False, skip_group_check=True)
                pe.matmul(banks[0][:, g * DIM:(g + 1) * DIM], featT[0:DIM, KT, :], w1[:, :], start=False, stop=True, skip_group_check=True)\
                  .then_inc(s_lm, 1)

        @block.vector
        def _(dve):
            steps = [0]

            def step(ins):
                steps[0] += 1
                ins.then_inc(s_prep, 1)
                dve.wait_ge(s_prep, steps[0])

            dve.memset(raw_rows[:, FULL:COLS], BLOCKS * P).then_inc(s_tail, 1)
            dve.memset(raw_cols[:, FULL:COLS], 0).then_inc(s_tail, 1)
            dve.memset(raw_vals[:, FULL:COLS], 0.0).then_inc(s_tail, 1)
            dve.memset(srt[:, :, :], 0.0).then_inc(s_vconst, 1)
            dve.memset(zero_b[:, :], 0.0).then_inc(s_vconst, 1)
            dve.wait_ge(s_batch, 32)
            mark = sem("s_rchain")
            n = [0]

            def rstep(ins):
                n[0] += 1
                ins.then_inc(mark, 1)
                dve.wait_ge(mark, n[0])
            for side, size in ((0, N_USERS), (1, N_ITEMS)):
                rstep(dve.tensor_copy(r_f[:, side, :], r_i[:, side, :]))
                rstep(dve.tensor_scalar(r_neg[:, side, :], r_f[:, side, :], 0.0, float(size), ALU.is_lt, ALU.mult))
                rstep(dve.tensor_tensor(r_c[:, side, :], r_f[:, side, :], r_neg[:, side, :], ALU.add))
                rstep(dve.tensor_scalar(r_f[:, side, :], r_c[:, side, :], 0.0, float(size - 1), ALU.max, ALU.min))
                rstep(dve.tensor_copy(r_idx[:, side, :], r_f[:, side, :]))
                rstep(dve.tensor_scalar(n_f[:, side, :], r_f[:, side, :], float(N_USERS * side), None, ALU.add))
                rstep(dve.tensor_copy(n_i[:, side, :], n_f[:, side, :]))
            rstep(dve.tensor_scalar(n_lo[:, :, :], n_i[:, :, :], P - 1, None, ALU.bitwise_and))
            rstep(dve.tensor_scalar(n_hi[:, :, :], n_i[:, :, :], 7, None, ALU.arith_shift_right))
            rstep(dve.scalar_tensor_tensor(t_idx[:, :, :], n_lo[:, :, :], float(BUCKETS), n_hi[:, :, :], ALU.mult, ALU.add))
            rstep(dve.tensor_copy(n_lo_f[:, :, :], n_lo[:, :, :]))
            rstep(dve.tensor_copy(n_hi_f[:, :, :], n_hi[:, :, :]))
            dve.sem_inc(s_ridx, 1)
            dve.sem_inc(s_nf, 1)
            dve.wait_ge(s_const, 16)
            step(dve.tensor_copy(iota_b[:, :], iota_i[:, :]))
            step(dve.tensor_copy(iota_r[:, :], iota_i[:, 0:P]))
            step(dve.tensor_copy(tmap[:, :], tmap_i[:, :]))
            step(dve.tensor_copy(row_base[:, :], row_base_i[:, :]))
            step(dve.tensor_copy(part_node[:, :], part_node_i[:, :]))
            step(dve.tensor_copy(ident_h[:, :], ident[:, :]))
            for q in range(SLOTS):
                side, g = q // GROUPS, q % GROUPS
                if q >= 2:
                    dve.wait_ge(s_marked, q - 1)
                dve.tensor_scalar(mark_lo[:, q % 2, :], iota_b[:, 0:P], n_lo_f[:, side, g:g + 1], None, ALU.is_equal)
                dve.tensor_scalar(onehot[:, 0, q % 2, :], iota_b[:, :], n_hi_f[:, side, g:g + 1], None, ALU.is_equal).then_inc(s_mark, 1)
            dve.wait_ge(s_marked, SLOTS)
            step(dve.tensor_scalar(wanted[:, :], banks[5][:, 0:BUCKETS], 0.0, None, ALU.is_gt))
            dve.sem_inc(s_wanted, 1)
            dve.wait_ge(s_load, 96)
            step(dve.tensor_scalar(scratch_i, raw_rows, 7, None, ALU.arith_shift_right))
            step(dve.tensor_copy(hi, scratch_i))

            def one_hots(i, h, into):
                for s in range(STREAMS):
                    last = dve.tensor_scalar(onehot[:, h, s, :], iota_b[:, :], hi[:, bass.ds(i * 2 + (h + s * SCOLS), 1)], None, ALU.is_equal)
                last.then_inc(into[h], 1)

            step(dve.tensor_scalar(scratch_i, raw_rows, 7 + HC.bit_length() - 1, None, ALU.arith_shift_right))
            step(dve.tensor_copy(hi_a, scratch_i))
            step(dve.tensor_scalar(scratch_i, raw_rows, 7, HC - 1, ALU.arith_shift_right, ALU.bitwise_and))
            step(dve.tensor_copy(hi_c, scratch_i))
            step(dve.memset(ones_f[:, :], 1.0))
            step(dve.tensor_reduce(own_a[:, :], own_as[:, :, :], AX.X, ALU.add))
            dve.sem_inc(s_ones, 1)

            def histogram(i, st):
                here = bass.ds(i * HCOLS + st * SCOLS, HCOLS)
                for out_, values, n in ((is_a, hi_a, HA), (is_c, hi_c, HC)):
                    last = dve.tensor_tensor(out_[:, st, :, :], iota_b[:, 0:n].unsqueeze(1).to_broadcast([P, HCOLS, n]),
                                             values[:, here].unsqueeze(2).to_broadcast([P, HCOLS, n]), ALU.is_equal)
                last.then_inc(s_hoh[st], 1)
            for st in range(STREAMS):
                histogram(0, st)
            with dve.Fori(1, HSTEPS) as i:
                for st in range(STREAMS):
                    dve.wait_ge(s_hused[st], i)
                    histogram(i, st)
            step(dve.tensor_copy(rec[:, :, 0], raw_rows))
            step(dve.tensor_scalar(scratch_i, raw_cols, P - 1, None, ALU.bitwise_and))
            step(dve.tensor_scalar(raw_rows, raw_cols, 7, None, ALU.arith_shift_right))
            step(dve.scalar_tensor_tensor(rec[:, :, 2], scratch_i, float(BUCKETS), raw_rows, ALU.mult, ALU.add))
            step(dve.tensor_copy(rec[:, :, 1], raw_vals))
            dve.sem_inc(s_records, 1)
            HR = HG * HA
            for st in range(STREAMS):
                dve.wait_ge(s_hused[st], HSTEPS)
                dve.tensor_tensor(folded[0:HR, st, :, :], banks[st][0:HR, 0:HG * HC].rearrange("p (g c) -> p g c", c=HC), own_group[0:HR, :, :], ALU.mult)\
                   .then_inc(s_hfold, 1)
                dve.wait_ge(s_hfold, 2 * st + 1)
                dve.tensor_reduce(part_of[0:HR, st, :], folded[0:HR, st, :, :].rearrange("p g c -> p c g"), AX.X, ALU.add).then_inc(s_hfold, 1)
                dve.wait_ge(s_hfold, 2 * st + 2)
                if st >= 2:
                    dve.wait_ge(s_counted, st - 1)
                dve.tensor_tensor(spread_c[0:HR, st % 2, :, :], part_of[0:HR, st, :].unsqueeze(1).to_broadcast([HR, HA, HC]),
                                  own_a[0:HR, :].unsqueeze(2).to_broadcast([HR, HA, HC]), ALU.mult).then_inc(s_hspread, 1)
            dve.wait_ge(s_counted, STREAMS)
            step(dve.tensor_copy(base[:, 1, :], count[0]))
            for s in range(1, STREAMS):
                step(dve.tensor_tensor(base[:, s + 1, :], base[:, s, :], count[s], ALU.add))
            step(dve.tensor_scalar(cnt_i[:, :], base[:, STREAMS, :], float(P - 1), None, ALU.add))
            step(dve.tensor_scalar(nch_i[:, :], cnt_i[:, :], 7, None, ALU.arith_shift_right))
            step(dve.tensor_scalar(nch[:, :], nch_i[:, :], 1.0, None, ALU.max))
            step(dve.tensor_tensor_scan(ends[:, :], nch[:, :], zero_b[:, :], 0.0, ALU.add, ALU.add))
            step(dve.tensor_tensor(cnt[:, :], ends[:, :], nch[:, :], ALU.subtract))
            step(dve.tensor_scalar(base[:, 0, :], cnt[:, :], float(P), None, ALU.mult))
            for s in range(1, STREAMS):
                step(dve.tensor_tensor(base[:, s, :], base[:, s, :], base[:, 0, :], ALU.add))
            dve.sem_inc(s_base, 1)
            for j in range(MAPCOLS):
                step(dve.tensor_scalar(picked[:, :], ends[:, :], tmap[:, j:j + 1], 0.0, ALU.is_le, ALU.add, accum_out=blk[:, j:j + 1]))
            step(dve.tensor_scalar(first_16[:, :], blk[:, :], float(BUCKETS - 1), float(P), ALU.min, ALU.mult))
            dve.sem_inc(s_mapo, 1)

            pchain = [0]

            def places(i, h, first, nth):
                for s in range(STREAMS):
                    dve.wait_ge(s_rank[h], i * STREAMS + s + 1)
                    if s:
                        dve.wait_ge(s_read[h], i * STREAMS + s)
                    dve.scalar_tensor_tensor(picked[:, :], iota_b[:, :], hi[:, bass.ds(i * 2 + (h + s * SCOLS), 1)], count[s],
                                             ALU.is_equal, ALU.mult, accum_out=pos[:, h, s:s + 1]).then_inc(s_read[h], 1)
                dve.wait_ge(s_read[h], i * STREAMS + STREAMS)
                dve.tensor_copy(pos_i[:, h, :], pos[:, h, :]).then_inc(s_pc, 1)
                dve.wait_ge(s_pc, nth * 3 + 1)
                dve.tensor_scalar(pos_lo[:, h, :], pos_i[:, h, :], P - 1, None, ALU.bitwise_and).then_inc(s_pc, 1)
                dve.tensor_scalar(pos_hi[:, h, :], pos_i[:, h, :], 7, None, ALU.arith_shift_right).then_inc(s_pc, 1)
                dve.wait_ge(s_pc, nth * 3 + 3)
                if not first:
                    dve.wait_ge(s_scat[h], i * (16 * STREAMS))
                dve.scalar_tensor_tensor(pos_out[:, h, :], pos_lo[:, h, :], float(CHUNKS), pos_hi[:, h, :], ALU.mult, ALU.add)\
                   .then_inc(s_pos[h], 1)

            for st in range(STREAMS):
                dve.wait_ge(s_hused[st], HSTEPS)
            one_hots(0, 0, s_roh)
            one_hots(0, 1, s_roh)
            places(0, 0, True, 0)
            dve.wait_ge(s_rused[0], 1)
            one_hots(1, 0, s_roh)
            places(0, 1, True, 1)
            dve.wait_ge(s_rused[1], 1)
            one_hots(1, 1, s_roh)
            places(1, 0, False, 2)
            with dve.Fori(2, SBODIES) as i:
                dve.wait_ge(s_rused[0], i)
                one_hots(i, 0, s_roh)
                places(i - 1, 1, False, i * 2 - 1)
                dve.wait_ge(s_rused[1], i)
                one_hots(i, 1, s_roh)
                places(i, 0, False, i * 2)
            places(SBODIES - 1, 1, False, 2 * SBODIES - 1)

            def selectors(l, k, h):
                dve.wait_ge(s_prod[l][h], k + 1)
                here = bass.ds(k * (2 * HALF) + h * HALF, HALF)
                dve.tensor_tensor(low[:, h, :], srt[:, here, 0], first[:, here], ALU.subtract).then_inc(s_low, 1)
                dve.wait_ge(s_val[l][h], k + 1)
                dve.wait_ge(s_low, k * 2 + (2 * BODIES * l + h + 1))
                for j in range(HALF):
                    last = dve.tensor_scalar(sel[:, h, j, :], iota_r[:, :], low[:, h, j:j + 1], val[:, h, j:j + 1], ALU.is_equal, ALU.mult)
                last.then_inc(s_sel[l][h], 1)

            def add_products(l, k, h):
                at = dve.value_load(window[0:1, bass.ds(k * 2 + h, 1)], min_val=0, max_val=(BUCKETS - 1) * DIM)
                dve.wait_ge(s_prod[l][h], k + 2)
                dve.wait_ge(s_add, k * 2 + (2 * BODIES * l + h + CREDIT))
                dst = acc[:, bass.ds(at, HALF * DIM)]
                dve.tensor_tensor(dst, dst, banks[h][:, :], ALU.add).then_inc(s_add, 1)
                dve.wait_ge(s_add, k * 2 + (2 * BODIES * l + h + 1 + CREDIT))
                dve.sem_inc(s_free[l][h], 1)

            def look_up(q):
                for b in range(2):
                    here = bass.ds(q * (2 * HALF) + b * HALF, HALF)
                    dve.wait_ge(s_turned[b], q + 1)
                    dve.tensor_tensor(look_low[:, b, :], srt[:, here, 0], first[:, here], ALU.subtract).then_inc(s_llow, 1)
                    dve.wait_ge(s_llow, q * 2 + (b + 1))
                    for j in range(HALF):
                        last = dve.tensor_scalar(look[:, b, j, :], iota_b[:, 0:P], look_low[:, b, j:j + 1], None, ALU.is_equal)
                    last.then_inc(s_look[b], 1)

            dve.wait_ge(s_srt, 16)
            dve.wait_ge(s_map, 32)
            by_half = first[0:1, :].rearrange("p (n j) -> p n j", j=HALF)
            dve.tensor_tensor(first_d[0:1, :].rearrange("p (n j) -> p n j", j=HALF), by_half,
                              by_half[:, :, 0:1].to_broadcast([1, CHUNKS // HALF, HALF]), ALU.subtract).then_inc(s_win, 1)
            dve.wait_ge(s_win, 1)
            dve.tensor_scalar(ahead[:, :], first_d[0:1, :], DIM / P, None, ALU.mult).then_inc(s_win, 1)
            dve.tensor_scalar(window[:, :], by_half[:, :, 0], DIM / P, None, ALU.mult).then_inc(s_win, 1)
            dve.wait_ge(s_win, 3)
            dve.sem_inc(s_windows, 1)
            for h in range(2):
                dve.wait_ge(s_rused[h], SBODIES)
            for n in range(TS):
                if n >= 2:
                    dve.wait_ge(s_expanded, n - 1)
                for c in range(KB):
                    last = dve.tensor_scalar(bucket_is[0:BP, n % 2, c, :], first[0:BP, n * TW:(n + 1) * TW], part_node[0:BP, c:c + 1], None, ALU.is_equal)
                last.then_inc(s_expand, 1)
            dve.wait_ge(s_expanded, TS)
            for l in range(LAYERS - 1):
                if l:
                    dve.wait_ge(s_tab, 16 * l)
                dve.memset(acc[:, :], 0.0).then_inc(s_zacc, 1)
                for h in range(2):
                    dve.sem_inc(s_free[l][h], 1)
                dve.wait_ge(s_zacc, l + 1)
                if l == 0:
                    dve.sem_inc(s_add, CREDIT)
                selectors(l, 0, 0)
                selectors(l, 0, 1)
                if l == 0:
                    look_up(0)
                    with dve.Fori(0, LOOK_BODIES - 1) as k:
                        for h in range(2):
                            add_products(l, k, h)
                            selectors(l, k + 1, h)
                            look_up(k * 2 + (h + 1))
                    for h in range(2):
                        add_products(l, LOOK_BODIES - 1, h)
                        selectors(l, LOOK_BODIES, h)
                        if h == 0:
                            look_up(SETS - 1)
                with dve.Fori(LOOK_BODIES if l == 0 else 0, BODIES - 1) as k:
                    for h in range(2):
                        add_products(l, k, h)
                        selectors(l, k + 1, h)
                for h in range(2):
                    add_products(l, BODIES - 1, h)

            nn = [0]

            def nstep(ins):
                nn[0] += 1
                ins.then_inc(s_near, 1)
                dve.wait_ge(s_near, nn[0])
            dve.wait_ge(s_tab, 16 * (LAYERS - 1))
            nstep(dve.memset(zero_t, 0.0))
            nstep(dve.tensor_reduce(near, flags[:, :], AX.X, ALU.add))
            dve.wait_ge(s_nearT, 1)
            nstep(dve.tensor_reduce(rounds_f[0:1, 0:1], banks[4][0:1, 0:P], AX.X, ALU.max))
            nstep(dve.tensor_scalar(rounds_f[0:1, 1:2], rounds_f[0:1, 0:1], 15.0, 16.0, ALU.add, ALU.max))
            nstep(dve.tensor_copy(rounds_i[0:1, 1:2], rounds_f[0:1, 1:2]))
            nstep(dve.tensor_scalar(rounds_i[0:1, 0:1], rounds_i[0:1, 1:2], 4, None, ALU.arith_shift_right))
            dve.sem_inc(s_rounds, 1)
            turns = dve.value_load(rounds_i[0:1, 0:1], min_val=1, max_val=CHUNKS // 8)
            chunk_no = match[:, 0:2, :].rearrange("p a n -> p (a n)")[:, 0:CHUNKS]
            nstep(dve.memset(keys, 1.0))
            nstep(dve.tensor_tensor_scan(chunk_no, keys, flags[:, :], 0.0, ALU.add, ALU.bypass) if 0 else
                  dve.tensor_tensor_scan(chunk_no, keys, zero_t[:, 0:1].to_broadcast([P, CHUNKS]), 0.0, ALU.add, ALU.add))
            nstep(dve.tensor_scalar(chunk_no, chunk_no, -1.0, float(CHUNKS + 1), ALU.mult, ALU.add))
            nstep(dve.tensor_tensor(keys, chunk_no, flags[:, :], ALU.mult))
            dve.wait_ge(s_nodes, 32)
            nstep(dve.tensor_copy(nodes, nodes_in.rearrange("p (u q) -> p q u", q=SLOTS)))

            def pick(r, b):
                STEPS = 5
                at = r * (2 * STEPS) + b * STEPS
                dve.nop(nofuse=True)
                dve.max(top, keys).then_inc(s_top, 1)
                dve.wait_ge(s_top, at + 1)
                dve.scalar_tensor_tensor(keys, keys, top[:, 7:8], keys, ALU.is_lt, ALU.mult).then_inc(s_top, 1)
                dve.tensor_scalar(valid[:, b, :], top, 0.0, None, ALU.is_gt).then_inc(s_top, 1)
                dve.tensor_scalar(at_f, top, -1.0, float(CHUNKS), ALU.mult, ALU.add).then_inc(s_top, 1)
                dve.wait_ge(s_top, at + 4)
                dve.tensor_scalar(at_i, at_f, float(CHUNKS - 1), row_base[:, :], ALU.min, ALU.add).then_inc(s_at, 1)
                dve.wait_ge(s_found, r * (2 * 16 * 8) + (b + 1) * 16 * 8)
                dve.tensor_tensor(val8[:, b, :], found[:, b, :, 1], valid[:, b, :], ALU.mult).then_inc(s_top, 1)
                dve.tensor_copy(src_i[:, b, :], found[:, b, :, 2]).then_inc(s_src, 1)
                dve.wait_ge(s_top, at + STEPS)

            def compare(r, b):
                for j in range(8):
                    dve.wait_ge(s_matched[j % 2], r * 8 + (b * 4 + j // 2 + 1))
                    dve.tensor_scalar(match[:, j % 2, :], nodes.rearrange("p q u -> p (q u)"), found[:, b, j, 0:1], val8[:, b, j:j + 1],
                                      ALU.is_equal, ALU.mult).then_inc(s_match[j % 2], 1)
            with dve.Fori(0, turns) as r:
                pick(r, 0)
                pick(r, 1)
                compare(r, 0)
                compare(r, 1)
                for i in range(2):
                    dve.wait_ge(s_matched[i], r * 8 + 9)

            dve.wait_ge(s_lm, 1)
            dve.tensor_copy(phi4T[:, :, :].rearrange("k c d -> k (c d)"), banks[2][0:KS, :]).then_inc(s_lmc, 1)
            dve.wait_ge(s_lm, 2)
            dve.tensor_scalar(w1[:, :], banks[3][0:DIM, 0:DIM], 0.1, None, ALU.mult).then_inc(s_lmc, 1)
            dve.tensor_scalar(ulm9[:, :, :], ulm[:, :, :], 0.9, None, ALU.mult).then_inc(s_lmc, 1)
            for g in range(GROUPS):
                if g:
                    dve.wait_ge(s_lm, 2 + g)
                dve.wait_ge(s_ft, g + 1)
                dve.tensor_copy(featT[0:KS, 0:4, :].rearrange("k c u -> k (c u)"), banks[4][0:KS, :])
                dve.tensor_copy(featT[0:KS, 4:8, :].rearrange("k c u -> k (c u)"), banks[5][0:KS, :])
                dve.tensor_copy(featT[0:DIM, KT, :], banks[1][0:DIM, 0:P]).then_inc(s_ftc, 1)
            dve.wait_ge(s_lm, 2 + GROUPS)
            dve.tensor_tensor(user_lm[:, :, :].rearrange("p g d -> p (g d)"), banks[0][:, :],
                              ilm_g[:, :, :].rearrange("p g d -> p (g d)"), ALU.mult).then_inc(s_lmc, 1)
            dve.wait_ge(s_lmc, 4)
            dve.tensor_reduce(gamma_lm[:, :], user_lm[:, :, :], AX.X, ALU.add).then_inc(s_lmc, 1)
            dve.wait_ge(s_light, 16 * SLOTS * LAYERS)
            dve.tensor_reduce(light[:, :, :].rearrange("p n d -> p (n d)"), tabs_g.rearrange("p l n d -> p (n d) l"), AX.X, ALU.add).then_inc(s_fold, 1)
            dve.wait_ge(s_fold, 1)
            for side in range(2):
                half = light[:, side * GROUPS:(side + 1) * GROUPS, :].rearrange("p n d -> p (n d)")
                last = dve.tensor_tensor(half, half, banks[6 + side][:, :], ALU.add)
            last.then_inc(s_lmc, 1)
            dve.wait_ge(s_lmc, 6)
            dve.tensor_tensor(user_lm[:, :, :], light[:, 0:GROUPS, :], light[:, GROUPS:2 * GROUPS, :], ALU.mult).then_inc(s_lmc, 1)
            dve.wait_ge(s_lmc, 7)
            dve.tensor_reduce(gamma_id[:, :], user_lm[:, :, :], AX.X, ALU.add).then_inc(s_lmc, 1)
            dve.wait_ge(s_lmc, 8)
            dve.scalar_tensor_tensor(result[:, :], gamma_id[:, :], 0.5 / (LAYERS + 1) ** 2, gamma_lm[:, :], ALU.mult, ALU.add)\
               .then_inc(s_fin, 1)


_INS = ['r_users', 'r_items', 'L0_rec_user_emb', 'L0_rec_item_emb', 'L0_rec_rows', 'L0_rec_cols', 'L0_rec_vals',
        'L0_rec_phi3', 'L0_rec_phi4', 'L0_rec_phi2', 'L0_rec_user_lm_T', 'L0_rec_item_lm']


def kernel(**inputs):
    import numpy as _np
    import concourse.bacc as _bacc
    from concourse import mybir as _mybir
    from concourse.bass_utils import run_bass_kernel_spmd as _run

    nc = _bacc.Bacc("TRN2", target_bir_lowering=False, num_devices=1)
    arrays, args = {}, []
    for name in _INS:
        a = _np.ascontiguousarray(inputs[name])
        arrays[f"in_{name}"] = a
        args.append(nc.dram_tensor(f"in_{name}", a.shape, _mybir.dt.from_np(a.dtype), kind="ExternalInput").ap())
    batch = arrays["in_r_users"].shape[0]
    out = nc.dram_tensor("out_scores", (batch,), _mybir.dt.float32, kind="ExternalOutput").ap()
    rec_kernel(nc, *args, out)
    r = _run(nc, [arrays], core_ids=[0])
    return r.results[0]["out_scores"]
```

```python
import numpy as np
import concourse.bass as bass
from concourse import mybir
from contextlib import ExitStack

"""LightGCN propagation (three sparse matrix products) and batch scores.

The edges are sorted on the chip by the 128-node block of their row (a counting sort: a histogram, then
each edge's rank by one-hot matrix products, then an indirect scatter).  A layer then walks the sorted
edges in chunks of 128 that all lie in one block: GpSimd gathers the chunk's source rows, TensorE
multiplies them with a [edge, row-in-block] matrix that holds the edge's value (its product sums the edges
of each row), and VectorE adds the product to the block's accumulator in SBUF.

Only the batch's rows are asked for.  So the last layer takes just the edges whose row is in the batch,
and layer 2 just those whose row is in the batch or is a column of such an edge.  While layer 1 runs, two
passes look each edge's row up in a table of wanted nodes: the first finds the batch's edges, whose columns
are then marked too, and the second finds layer 2's edges.  Those are packed into fewer chunks in front of
layer 2.  Loops over them take their counts from registers, up to every edge.

Node n is at partition n % 128, block n // 128 on chip, and at row (n % 128) * BUCKETS + n // 128 of the
embedding tables in DRAM, so that the accumulators go out in one contiguous run per partition.
"""


def rec_kernel(nc, r_users, r_items, user_emb, item_emb, rows, cols, vals, phi3, phi4, phi2, user_lm_T,
               item_lm, out):
    f32, f16, i32, i16 = mybir.dt.float32, mybir.dt.float16, mybir.dt.int32, mybir.dt.int16
    bf16 = mybir.dt.bfloat16
    ALU = mybir.AluOpType
    ACT = mybir.ActivationFunctionType
    AX = mybir.AxisListType

    P = 128
    N_USERS, DIM = user_emb.shape
    N_ITEMS = item_emb.shape[0]
    N_NODES = N_USERS + N_ITEMS
    NNZ = rows.shape[0]
    BATCH = r_users.shape[0]
    M_PHI = phi2.shape[1]
    LAYERS = 3
    STAGES = 3

    BLOCKS = -(-N_NODES // P)
    BUCKETS = BLOCKS + 1
    STREAMS = 5
    FULL = NNZ // P
    TAIL = NNZ - FULL * P
    HC = 16
    HA = -(-BUCKETS // HC)
    HG = P // HA
    SCOLS = -(-(FULL + 1) // (2 * HG * STREAMS)) * 2 * HG
    HM = next(m for m in range(8, 0, -1) if SCOLS // HG % m == 0)
    HCOLS = HM * HG
    HSTEPS = SCOLS // HCOLS
    COLS = SCOLS * STREAMS
    SBODIES = SCOLS // 2
    HALF = 8
    SETS = -(-((COLS * P + BUCKETS * P) // P) // (4 * HALF)) * 2
    CHUNKS = SETS * 2 * HALF
    LOOK_BODIES = SETS // 2
    BODIES = CHUNKS // (2 * HALF)
    MAPCOLS = -(-CHUNKS // P)
    GROUPS = BATCH // P
    SLOTS = 2 * GROUPS
    KT = 8
    CREDIT = 2
    KS = M_PHI // KT

    tables = [nc.dram_tensor(f"table{l}", (P * BUCKETS, DIM), f32, kind="Internal").ap() for l in range(LAYERS)]
    sorted_dram = nc.dram_tensor("sorted_edges", (P * CHUNKS, 3), f32, kind="Internal").ap()
    kept_dram = nc.dram_tensor("kept_edges", (P * CHUNKS + P * 2 * HALF, 3), f32, kind="Internal").ap()
    flags_dram = nc.dram_tensor("batch_flags", (P * CHUNKS,), f16, kind="Internal").ap()
    first_dram = nc.dram_tensor("chunk_first_node", (MAPCOLS * P,), f16, kind="Internal").ap()
    nodes_dram = nc.dram_tensor("batch_nodes", (P * SLOTS,), f32, kind="Internal").ap()

    ctx = ExitStack()
    with ctx:
        def sb(name, shape, dt=f32):
            return ctx.enter_context(nc.sbuf_tensor(name, shape, dt))

        def pb(name, shape, dt=f32):
            return ctx.enter_context(nc.psum_tensor(name, shape, dt))

        def sem(name):
            return ctx.enter_context(nc.semaphore(name))

        acc = sb("acc", [P, (BUCKETS + HALF - 1) * DIM])
        raw_rows = acc[:, 0:COLS].bitcast(i32)
        raw_cols = acc[:, COLS:2 * COLS].bitcast(i32)
        raw_vals = acc[:, 2 * COLS:3 * COLS]
        scratch_i = acc[:, 3 * COLS:4 * COLS].bitcast(i32)
        hi = acc[:, 4 * COLS:5 * COLS]
        hi_a = acc[:, 5 * COLS:5 * COLS + COLS // 2].bitcast(f16)
        hi_c = acc[:, 5 * COLS + COLS // 2:6 * COLS].bitcast(f16)
        rec = sb("rec", [P, COLS, 3])
        rec_s = rec[:, :, :].rearrange("p (s c) f -> p s c f", s=STREAMS)
        srt = sb("srt", [P, CHUNKS, 3])
        phi2_g = srt[:, :, :].rearrange("p c f -> p (c f)")[:, 0:GROUPS * M_PHI].rearrange("p (g m) -> p g m", g=GROUPS)

        def carver(flat):
            at = [0]

            def carve(shape, dt=f32):
                width = int(np.prod(shape[1:]))
                words = width if dt not in (f16, bf16) else -(-width // 2)
                part = flat[0:shape[0], at[0]:at[0] + words]
                at[0] += words
                assert at[0] <= flat.shape[1]
                if dt != f32:
                    part = part.bitcast(dt)
                if len(shape) == 2:
                    return part
                names = "abc"[:len(shape) - 1]
                return part.rearrange(f"p ({' '.join(names)}) -> p {' '.join(names)}", **dict(zip(names, shape[1:])))
            return carve

        after_sort = carver(rec[:, :, :].rearrange("p c f -> p (c f)"))
        after_layers = carver(acc[:, :])
        in_layer = carver(rec[:, :, :].rearrange("p c f -> p (c f)"))
        to_keep_r = carver(rec[:, :, :].rearrange("p c f -> p (c f)"))
        to_keep_s = carver(srt[:, :, :].rearrange("p c f -> p (c f)"))
        room = sb("room", [P, 5 * P * HALF + 256])
        for_sort = carver(room[:, :])
        for_layers = carver(room[:, :])

        KB = 3
        BP = BUCKETS // KB
        TS = 8
        TW = CHUNKS // TS
        for_hist = carver(room[:, :])
        is_a = for_hist([P, STREAMS, HCOLS, HA], f16)
        is_c = for_hist([P, STREAMS, HCOLS, HC], f16)
        folded = for_hist([P, STREAMS, HG, HC])
        part_of = for_hist([P, STREAMS, HC])
        spread_c = for_hist([P, 2, HA, HC])
        own_group = for_hist([P, HG, HC])
        own_as = for_hist([P, HA, HG])
        own_a = for_hist([P, HA])
        iota_i = sb("iota_i", [P, BUCKETS], i32)
        iota_b = sb("iota_b", [P, BUCKETS], f16)
        iota_r = sb("iota_r", [P, P])
        tmap_i = sb("tmap_i", [P, MAPCOLS], i32)
        tmap = sb("tmap", [P, MAPCOLS])
        tmap_half = sb("tmap_half", [P, MAPCOLS])
        ident = sb("ident", [P, P])
        assert CHUNKS % 8 == 0 and BUCKETS % 3 == 0
        ident_h = sb("ident_h", [P, P], f16)
        ones = sb("ones", [P, P], f16)
        below = sb("below", [P, P], f16)
        rest = sb("rest", [P, P], f16)
        onehot = for_sort([P, 2, STREAMS, BUCKETS], f16)
        picked = for_sort([P, BUCKETS])
        pos = sb("pos", [P, 2, STREAMS])
        pos_i = sb("pos_i", [P, 2, STREAMS], i32)
        pos_lo = sb("pos_lo", [P, 2, STREAMS], i32)
        pos_hi = sb("pos_hi", [P, 2, STREAMS], i32)
        pos_out = sb("pos_out", [P, 2, STREAMS], i32)
        rec_out = sb("rec_out", [P, 2, STREAMS, 3])
        bucket_is = onehot[:, :, :, :].rearrange("p a s b -> p (a s b)")[:, 0:2 * KB * TW].rearrange("p (a c t) -> p a c t", a=2, c=KB)
        base = for_sort([P, STREAMS + 1, BUCKETS])
        cnt = for_sort([P, BUCKETS])
        cnt_i = for_sort([P, BUCKETS], i32)
        nch_i = for_sort([P, BUCKETS], i32)
        nch = for_sort([P, BUCKETS])
        ends = for_sort([P, BUCKETS])
        zero_b = sb("zero_b", [P, BUCKETS])
        blk = sb("blk", [P, MAPCOLS])
        half_f = sb("half_f", [1, 2])
        half_i = sb("half_i", [1, 5], i32)
        first_16 = sb("first_16", [P, MAPCOLS], f16)
        ahead = sb("ahead", [1, CHUNKS], i16)
        first_d = acc[:, 0:CHUNKS]
        window = sb("window", [1, CHUNKS // HALF], i32)
        first = sb("first", [P, CHUNKS], f16)
        ones_f = sb("ones_f", [P, P])
        zero_h = sb("zero_h", [P, P], f16)
        zero_w = sb("zero_w", [P, HALF * DIM], f16)
        val = sb("val", [P, 2, HALF])
        part_node_i = sb("part_node_i", [P, KB], i32)
        part_node = sb("part_node", [P, KB])
        wantedT = sb("wantedT", [BP, KB, P], f16)
        wanted_at = sb("wanted_at", [P, CHUNKS], f16)
        low = sb("low", [P, 2, HALF])
        flags = sb("flags", [P, CHUNKS], f16)
        wanted = sb("wanted", [P, BUCKETS], f16)
        wanted_8 = sb("wanted_8", [P, 2, HALF], f16)
        look_low = sb("look_low", [P, 2, HALF])
        look = for_layers([P, 2, HALF, P], f16)
        lookT = for_layers([P, 2, HALF, P], f16)
        a_keys = in_layer([P, CHUNKS])
        a_bucket_is = in_layer([P, 2, KB, TW], f16)
        a_lo = in_layer([P, 8, P], f16)
        a_hi = in_layer([P, 8, BUCKETS], f16)
        a_steps = in_layer([P, P])
        a_step_i = in_layer([P, P], i32)
        a_le = in_layer([P, P], f16)
        a_top = in_layer([P, 8])
        a_valid = in_layer([P, 8])
        a_at_f = in_layer([P, 8])
        a_at_i = in_layer([P, 8], i32)
        a_found = in_layer([P, 8, 3])
        a_tab = in_layer([P, 8])
        a_lo_n = in_layer([P, 8])
        a_lo_m = in_layer([P, 8])
        a_hi_n = in_layer([P, 8])
        a_near = in_layer([P, 1])
        a_rounds_f = in_layer([1, 4])
        a_rounds_i = in_layer([1, 2], i32)
        k_col = to_keep_s([P, CHUNKS])
        k_rank = to_keep_s([P, CHUNKS])
        k_same = to_keep_s([P, CHUNKS])
        k_c = to_keep_r([P, CHUNKS])
        k_d = to_keep_r([P, CHUNKS])
        k_top = to_keep_r([P, 2, 8])
        k_at_u = to_keep_r([P, 2, 8], mybir.dt.uint32)
        k_at_f = to_keep_r([P, 2, 8])
        k_at_i = to_keep_r([P, 2, 8], i32)
        k_valid = to_keep_r([P, 2, 8])
        k_pos = to_keep_r([P, 2, 8], i32)
        k_lo = to_keep_r([P, 2, 8], i32)
        k_hi = to_keep_r([P, 2, 8], i32)
        k_row = to_keep_r([P, 2, 8])
        k_row_v = to_keep_r([P, 2, 8])
        k_dst = to_keep_r([P, 2, 8], i32)
        k_found = to_keep_r([P, 2, 8, 3])
        k_trash_i = to_keep_r([P, 2 * 8], i32)
        k_trash = to_keep_r([P, 2, 8])
        k_near = to_keep_r([P, 1])
        k_rounds_f = to_keep_r([1, 4])
        k_rounds_i = to_keep_r([1, 2], i32)
        k_bodies_f = to_keep_r([1, 4])
        k_bodies_i = to_keep_r([1, 4], i32)
        row_base = sb("row_base", [P, 1])
        row_base_i = sb("row_base_i", [P, 1], i32)
        nodes_in = after_layers([P, P * SLOTS])
        nodes = nodes_in.rearrange("p (u q) -> p q u", q=SLOTS)
        match = after_layers([P, 2, SLOTS * P], bf16)
        left = after_layers([P, 2, 8, DIM])
        parts = after_layers([P, 3, 2 * 8, DIM], bf16)
        source = after_layers([P, 2, 8, DIM])
        tabs2_g = after_layers([P, SLOTS, DIM])
        light = after_layers([P, SLOTS, DIM])
        phi3_g = after_sort([P, GROUPS, DIM])
        ilm_g = after_sort([P, GROUPS, DIM])
        phi4_sb = after_sort([DIM, M_PHI])
        ulm = after_sort([KS, KT, DIM])
        phi4T = after_sort([KS, KT, DIM])
        ulm9 = after_sort([KS, KT, DIM])
        keys = after_sort([P, CHUNKS])
        top = after_sort([P, 2, 8])
        valid = after_sort([P, 2, 8])
        at_f = after_sort([P, 2, 8])
        at_i = after_sort([P, 2, 8], i32)
        src_i = after_sort([P, 2, 8], i32)
        val8 = after_sort([P, 2, 8])
        found = after_sort([P, 2, 8, 3])
        near = after_sort([P, 1])
        rounds_f = after_sort([1, 4])
        rounds_i = after_sort([1, 2], i32)
        in_room = carver(room[:, :])
        tabs_g = in_room([P, LAYERS - 1, SLOTS, DIM])
        featT = in_room([P, 2, KT + 1, P])
        w1 = in_room([DIM, DIM])
        user_lm = in_room([P, GROUPS, DIM])
        idx = sb("idx", [P, 2, HALF], i32)
        got = for_layers([P, 2, HALF, DIM])
        sel = for_layers([P, 2, HALF, P])

        r_i = sb("r_i", [P, 2, GROUPS], i32)
        r_f = sb("r_f", [P, 2, GROUPS])
        r_neg = sb("r_neg", [P, 2, GROUPS])
        r_c = sb("r_c", [P, 2, GROUPS])
        r_idx = sb("r_idx", [P, 2, GROUPS], i32)
        n_f = sb("n_f", [P, 2, GROUPS])
        n_lo_f = sb("n_lo_f", [P, 2, GROUPS])
        n_hi_f = sb("n_hi_f", [P, 2, GROUPS])
        mark_lo = sb("mark_lo", [P, 2, P], f16)
        n_i = sb("n_i", [P, 2, GROUPS], i32)
        n_lo = sb("n_lo", [P, 2, GROUPS], i32)
        n_hi = sb("n_hi", [P, 2, GROUPS], i32)
        t_idx = sb("t_idx", [P, 2, GROUPS], i32)
        gamma_lm = sb("gamma_lm", [P, GROUPS])
        gamma_id = sb("gamma_id", [P, GROUPS])
        result = sb("result", [P, GROUPS])
    
        banks = [pb(f"bank{i}", [P, 512]) for i in range(8)]
        count = [banks[s][:, 0:BUCKETS] for s in range(STREAMS)]

        s_load = sem("s_load")
        s_tab0 = sem("s_tab0")
        s_batch = sem("s_batch")
        s_lmw = sem("s_lmw")
        s_const = sem("s_const")
        s_vconst = sem("s_vconst")
        s_tail = sem("s_tail")
        s_prep = sem("s_prep")
        s_records = sem("s_records")
        s_lmg = sem("s_lmg")
        s_hoh = [sem(f"s_hoh{st}") for st in range(STREAMS)]
        s_hused = [sem(f"s_hused{st}") for st in range(STREAMS)]
        s_hfold = sem("s_hfold")
        s_hspread = sem("s_hspread")
        s_counted = sem("s_counted")
        s_ones = sem("s_ones")
        s_zsrt = sem("s_zsrt")
        s_base = sem("s_base")
        s_roh = [sem(f"s_roh{h}") for h in range(2)]
        s_rank = [sem(f"s_rank{h}") for h in range(2)]
        s_read = [sem(f"s_read{h}") for h in range(2)]
        s_rused = [sem(f"s_rused{h}") for h in range(2)]
        s_recs = [sem(f"s_recs{h}") for h in range(2)]
        s_pos = [sem(f"s_pos{h}") for h in range(2)]
        s_pc = sem("s_pc")
        s_scat = [sem(f"s_scat{h}") for h in range(2)]
        s_mapo = sem("s_mapo")
        s_map = sem("s_map")
        s_srt = sem("s_srt")
        s_idx = [[sem(f"s_idx{l}{h}") for h in range(2)] for l in range(STAGES)]
        s_got = [[sem(f"s_got{l}{h}") for h in range(2)] for l in range(STAGES)]
        s_sel = [[sem(f"s_sel{l}{h}") for h in range(2)] for l in range(STAGES)]
        s_prod = [[sem(f"s_prod{l}{h}") for h in range(2)] for l in range(STAGES)]
        s_nodes = sem("s_nodes")
        s_nf = sem("s_nf")
        s_mark = sem("s_mark")
        s_marked = sem("s_marked")
        s_wanted = sem("s_wanted")
        s_look = [[sem(f"s_look{n}{b}") for b in range(2)] for n in range(2)]
        s_turned = [[sem(f"s_turned{n}{b}") for b in range(2)] for n in range(2)]
        s_lookT = [[sem(f"s_lookT{n}{b}") for b in range(2)] for n in range(2)]
        s_asked = [[sem(f"s_asked{n}{b}") for b in range(2)] for n in range(2)]
        s_flag = [[sem(f"s_flag{n}{b}") for b in range(2)] for n in range(2)]
        s_low = [sem(f"s_low{l}") for l in range(STAGES)]
        s_windows = sem("s_windows")
        s_expand = sem("s_expand")
        s_expanded = sem("s_expanded")
        s_wT = sem("s_wT")
        s_wTc = sem("s_wTc")
        s_wat = sem("s_wat")
        s_llow = [sem(f"s_llow{n}") for n in range(2)]
        s_fold = sem("s_fold")
        s_top = sem("s_top")
        s_at = sem("s_at")
        s_found = [sem(f"s_found{b}") for b in range(2)]
        s_src = sem("s_src")
        s_source = [sem(f"s_source{b}") for b in range(2)]
        s_match = [sem(f"s_match{h}") for h in range(2)]
        s_split = sem("s_split")
        s_matched = [sem(f"s_matched{h}") for h in range(2)]
        s_zacc = sem("s_zacc")
        s_half = sem("s_half")
        s_layer = sem("s_layer")
        s_a_near = sem("s_a_near")
        s_a_nearT = sem("s_a_nearT")
        s_a_rounds = sem("s_a_rounds")
        s_a_pick = sem("s_a_pick")
        s_a_at = sem("s_a_at")
        s_a_lo = sem("s_a_lo")
        s_a_found = sem("s_a_found")
        s_a_mark = sem("s_a_mark")
        s_a_marked = sem("s_a_marked")
        s_keep = sem("s_keep")
        s_k_const = sem("s_k_const")
        s_k_sums = sem("s_k_sums")
        s_k_read = sem("s_k_read")
        s_k_pick = sem("s_k_pick")
        s_k_dst = sem("s_k_dst")
        s_k_found = [sem(f"s_k_found{b}") for b in range(2)]
        s_put = [sem(f"s_put{b}") for b in range(2)]
        s_zkept = sem("s_zkept")
        s_slot = [sem(f"s_slot{b}") for b in range(2)]
        s_kept = sem("s_kept")
        s_k_map = sem("s_k_map")
        s_bodies = sem("s_bodies")
        s_add = [sem(f"s_add{l}") for l in range(STAGES)]
        s_tab = sem("s_tab")
        s_fin = sem("s_fin")
        s_light = sem("s_light")
        s_ft = sem("s_ft")
        s_ftc = sem("s_ftc")
        s_lm = sem("s_lm")
        s_lmc = sem("s_lmc")
        s_out = sem("s_out")

        block = ctx.enter_context(nc.Block())
        U0 = N_USERS // P
        UR = N_USERS - U0 * P
        I0 = P - UR
        IB = (N_ITEMS - I0) // P
        IR = N_ITEMS - I0 - IB * P

        @block.sync
        def _(sp):
            sp.wait_ge(s_tail, 3)
            for raw, dram in ((raw_rows, rows), (raw_cols, cols), (raw_vals, vals)):
                sp.dma_start(raw[:, 0:FULL], dram[0:FULL * P].rearrange("(p n) -> p n", p=P)).then_inc(s_load, 16)
                sp.dma_start(raw[0:TAIL, FULL:FULL + 1], dram[FULL * P:NNZ].rearrange("(p n) -> p n", n=1)).then_inc(s_load, 16)
            sp.dma_start(r_i[:, 0, :], r_users.rearrange("(p g) -> p g", g=GROUPS)).then_inc(s_batch, 16)
            sp.dma_start(r_i[:, 1, :], r_items.rearrange("(p g) -> p g", g=GROUPS)).then_inc(s_batch, 16)
            sp.wait_ge(s_nf, 1)
            sp.dma_start(nodes_dram.rearrange("(p q) -> p q", p=P), n_f[:, :, :].rearrange("p s g -> p (s g)")).then_inc(s_nodes, 16)
            sp.wait_ge(s_vconst, 1)
            sp.dma_start(sorted_dram.rearrange("(p c) f -> p (c f)", p=P),
                         srt[:, :, :].rearrange("p c f -> p (c f)")).then_inc(s_zsrt, 16)
            t0 = tables[0].rearrange("(p b) d -> p b d", p=P)
            sp.dma_start(t0[:, 0:U0, :], user_emb[0:U0 * P, :].rearrange("(b p) d -> p b d", p=P)).then_inc(s_tab0, 16)
            sp.dma_start(t0[0:UR, U0, :], user_emb[U0 * P:N_USERS, :]).then_inc(s_tab0, 16)
            sp.dma_start(t0[UR:P, U0, :], item_emb[0:I0, :]).then_inc(s_tab0, 16)
            sp.dma_start(t0[:, U0 + 1:U0 + 1 + IB, :], item_emb[I0:I0 + IB * P, :].rearrange("(b p) d -> p b d", p=P)).then_inc(s_tab0, 16)
            sp.dma_start(t0[0:IR, U0 + 1 + IB, :], item_emb[I0 + IB * P:N_ITEMS, :]).then_inc(s_tab0, 16)
            zeros = srt[:, :, :].rearrange("p c f -> p (c f)")[:, 0:DIM]
            sp.dma_start(t0[IR:P, U0 + 1 + IB, :], zeros[IR:P, :]).then_inc(s_tab0, 16)
            sp.dma_start(t0[:, BLOCKS, :], zeros).then_inc(s_tab0, 16)
            for b in range(2):
                sp.dma_start(kept_dram[0:P * CHUNKS, :].rearrange("(b p c) f -> b p (c f)", b=2, p=P)[b],
                             srt[:, :, :].rearrange("p c f -> p (c f)")[:, 0:CHUNKS * 3 // 2]).then_inc(s_zkept, 16)
            sp.wait_ge(s_mapo, 1)
            sp.dma_start(first_dram.rearrange("(p j) -> p j", p=P), first_16[:, :]).then_inc(s_map, 16)
            sp.wait_ge(s_map, 16)
            sp.dma_start(first[:, :], first_dram[0:CHUNKS].partition_broadcast(P)).then_inc(s_map, 16)
            for h in range(2):
                sp.wait_ge(s_scat[h], 16 * STREAMS * SBODIES)
            sp.wait_ge(s_tab0, 112)
            sp.wait_ge(s_zkept, 32)
            sp.dma_start(srt[:, :, :].rearrange("p c f -> p (c f)"),
                         sorted_dram.rearrange("(p c) f -> p (c f)", p=P)).then_inc(s_srt, 16)
            sp.wait_ge(s_half, 1)
            sets = sp.value_load(half_i[0:1, 3:4], min_val=4, max_val=SETS)
            for b in range(2):
                sp.wait_ge(s_flag[0][b], sets + 1)
            sp.dma_start(flags_dram.rearrange("(p c) -> p c", p=P), flags[:, :]).then_inc(s_keep, 16)
            for l in range(LAYERS - 1):
                sp.wait_ge(s_layer, l + 1)
                sp.dma_start(tables[l + 1].rearrange("(p b) d -> p (b d)", p=P), acc[:, 0:BUCKETS * DIM]).then_inc(s_tab, 16)
                if l == 0:
                    sp.wait_ge(s_mapo, 2)
                    sp.dma_start(first_dram.rearrange("(p j) -> p j", p=P), first_16[:, :]).then_inc(s_map, 16)
                    sp.wait_ge(s_map, 48)
                    sp.dma_start(first[:, :], first_dram[0:CHUNKS].partition_broadcast(P)).then_inc(s_map, 16)
                    sp.wait_ge(s_kept, 1)
                    sp.dma_start(srt[:, :, :].rearrange("p c f -> p (c f)"),
                                 kept_dram[0:P * CHUNKS, :].rearrange("(p c) f -> p (c f)", p=P)).then_inc(s_srt, 16)
                    sp.dma_start(flags[:, :], flags_dram.rearrange("(p c) -> p c", p=P)).then_inc(s_keep, 16)
                    sp.dma_start(phi4_sb, phi4).then_inc(s_lmw, 16)
                    sp.dma_start(ulm, user_lm_T.rearrange("(c k) d -> k c d", k=KS)).then_inc(s_lmw, 16)
            sp.wait_ge(s_tab, 16 * (LAYERS - 1))
            sp.wait_ge(s_nodes, 16)
            sp.dma_start(nodes_in, nodes_dram.partition_broadcast(P)).then_inc(s_nodes, 16)
            sp.wait_ge(s_fin, 1)
            sp.dma_start(out.rearrange("(p g) -> p g", g=GROUPS), result[:, :]).then_inc(s_out, 16)
            sp.wait_ge(s_out, 16)

        @block.gpsimd
        def _(pool):
            pool.iota(iota_i[:, :], pattern=[[1, BUCKETS]], base=0, channel_multiplier=0).then_inc(s_const, 1)
            pool.iota(tmap_i[:, :], pattern=[[1, MAPCOLS]], base=0, channel_multiplier=MAPCOLS).then_inc(s_const, 1)
            pool.memset(ones[:, :], 1.0).then_inc(s_const, 1)
            pool.memset(ident[:, :], 0.0).then_inc(s_const, 1)
            pool.iota(row_base_i[:, :], pattern=[[0, 1]], base=0, channel_multiplier=CHUNKS).then_inc(s_const, 1)
            pool.iota(part_node_i[:, :], pattern=[[P * BP, KB]], base=0, channel_multiplier=P).then_inc(s_const, 1)
            pool.memset(zero_h[:, :], 0.0).then_inc(s_const, 1)
            pool.memset(zero_w[:, :], 0.0).then_inc(s_const, 1)
            pool.memset(own_group[:, :, :], 1.0).then_inc(s_const, 1)
            pool.memset(own_as[:, :, :], 0.0).then_inc(s_const, 1)
            pool.wait_ge(s_const, 10)
            pool.affine_select(out=own_group[:, :, :], in_=own_group[:, :, :], compare_op=ALU.is_ge, fill=0.0,
                               base=0, pattern=[[-HA, HG], [0, HC]], channel_multiplier=1).then_inc(s_const, 1)
            pool.affine_select(out=own_as[:, :, :], in_=own_as[:, :, :], compare_op=ALU.not_equal, fill=1.0,
                               base=0, pattern=[[-1, HA], [-HA, HG]], channel_multiplier=1).then_inc(s_const, 1)
            pool.wait_ge(s_const, 12)
            pool.affine_select(out=own_group[:, :, :], in_=own_group[:, :, :], compare_op=ALU.is_ge, fill=0.0,
                               base=HA - 1, pattern=[[HA, HG], [0, HC]], channel_multiplier=-1).then_inc(s_const, 1)
            pool.affine_select(out=ident[:, :], in_=ident[:, :], compare_op=ALU.not_equal, fill=1.0,
                               base=0, pattern=[[-1, P]], channel_multiplier=1).then_inc(s_const, 1)
            pool.affine_select(out=below[:, :], in_=ones[:, :], compare_op=ALU.is_gt, fill=0.0,
                               base=0, pattern=[[1, P]], channel_multiplier=-1).then_inc(s_const, 1)
            pool.affine_select(out=rest[:, :], in_=ones[:, :], compare_op=ALU.is_ge, fill=0.0,
                               base=0, pattern=[[-1, P]], channel_multiplier=1).then_inc(s_const, 1)
            pool.wait_ge(s_zsrt, 16)
            with pool.Fori(0, SBODIES) as i:
                for h in range(2):
                    pool.wait_ge(s_recs[h], i + 1)
                    pool.wait_ge(s_pos[h], i + 1)
                    pool.nop(nofuse=True)
                    for s in range(STREAMS):
                        pool.indirect_dma_start(sorted_dram, bass.IndirectOffsetOnAxis(pos_out[:, h, s:s + 1], 0),
                                                rec_out[:, h, s, :], None).then_inc(s_scat[h], 16)
            pool.wait_ge(s_tab0, 112)

            def sources(l, k):
                for h in range(2):
                    pool.wait_ge(s_idx[l][h], k + 1)
                    pool.nop(nofuse=True)
                    for j in range(HALF):
                        pool.indirect_dma_start(got[:, h, j, :], None, tables[l // 2],
                                                bass.IndirectOffsetOnAxis(idx[:, h, j:j + 1], 0))\
                            .then_inc(s_got[l][h], 16)
            for h in range(2):
                pool.wait_ge(s_recs[h], SBODIES)
            pool.iota(a_step_i, pattern=[[BUCKETS, P]], base=1, channel_multiplier=0).then_inc(s_k_const, 1)
            pool.wait_ge(s_half, 1)
            half_steps = pool.value_load(half_i[0:1, 0:1], min_val=2, max_val=LOOK_BODIES)
            with pool.Fori(0, half_steps) as k:
                sources(0, k)
            sources(1, 0)
            pool.wait_ge(s_a_rounds, 1)
            turns = pool.value_load(a_rounds_i[0:1, 0:1], min_val=1, max_val=CHUNKS // 8)
            with pool.Fori(0, turns) as r:
                pool.wait_ge(s_a_at, r + 1)
                pool.nop(nofuse=True)
                for j in range(8):
                    pool.indirect_dma_start(a_found[:, j, :], None, sorted_dram,
                                            bass.IndirectOffsetOnAxis(a_at_i[:, j:j + 1], 0)).then_inc(s_a_found, 16)
            with pool.Fori(1, half_steps) as k:
                sources(1, k)
            pool.wait_ge(s_layer, 1)
            pool.iota(k_trash_i, pattern=[[1, 2 * HALF]], base=P * CHUNKS, channel_multiplier=2 * HALF).then_inc(s_k_const, 1)
            pool.wait_ge(s_a_rounds, 2)
            turns = pool.value_load(k_rounds_i[0:1, 0:1], min_val=1, max_val=CHUNKS // 8)
            pool.wait_ge(s_zkept, 32)
            for b in range(2):
                pool.sem_inc(s_slot[b], 1)
            with pool.Fori(0, turns) as r:
                for b in range(2):
                    pool.wait_ge(s_k_dst, r * 2 + (b + 1))
                    pool.wait_ge(s_slot[b], r + 1)
                    pool.nop(nofuse=True)
                    for j in range(8):
                        pool.indirect_dma_start(k_found[:, b, j, :], None, sorted_dram,
                                                bass.IndirectOffsetOnAxis(k_at_i[:, b, j:j + 1], 0)).then_inc(s_k_found[b], 16)
                for b in range(2):
                    pool.wait_ge(s_k_found[b], r * (16 * 8) + 16 * 8)
                    pool.nop(nofuse=True)
                    for j in range(8):
                        pool.indirect_dma_start(kept_dram, bass.IndirectOffsetOnAxis(k_dst[:, b, j:j + 1], 0),
                                                k_found[:, b, j, :], None).then_inc(s_put[b], 16)
                for b in range(2):
                    pool.wait_ge(s_put[b], r * (16 * 8) + 16 * 8)
                    pool.sem_inc(s_slot[b], 1)
            pool.sem_inc(s_kept, 1)
            pool.wait_ge(s_tab, 16)
            pool.wait_ge(s_bodies, 1)
            steps2 = pool.value_load(k_bodies_i[0:1, 0:1], min_val=2, max_val=BODIES)
            with pool.Fori(0, steps2) as k:
                sources(2, k)
            pool.wait_ge(s_layer, LAYERS - 1)
            for g in range(GROUPS):
                for dst, src, side in ((phi2_g, phi2, 0), (phi3_g, phi3, 0), (ilm_g, item_lm, 1)):
                    pool.indirect_dma_start(dst[:, g, :], None, src, bass.IndirectOffsetOnAxis(r_idx[:, side, g:g + 1], 0))\
                        .then_inc(s_lmg, 16)
            def batch_rows(l, dst):
                for side in range(2):
                    for g in range(GROUPS):
                        pool.indirect_dma_start(dst[:, side * GROUPS + g, :], None, tables[l],
                                                bass.IndirectOffsetOnAxis(t_idx[:, side, g:g + 1], 0)).then_inc(s_light, 16)
            batch_rows(0, tabs_g[:, 0, :, :])
            pool.wait_ge(s_a_rounds, 3)
            turns = pool.value_load(rounds_i[0:1, 0:1], min_val=1, max_val=CHUNKS // 8)
            with pool.Fori(0, turns) as r:
                for b in range(2):
                    pool.wait_ge(s_at, r * 2 + (b + 1))
                    pool.nop(nofuse=True)
                    for j in range(8):
                        pool.indirect_dma_start(found[:, b, j, :], None, sorted_dram,
                                                bass.IndirectOffsetOnAxis(at_i[:, b, j:j + 1], 0)).then_inc(s_found[b], 16)
                pool.wait_ge(s_tab, 16 * (LAYERS - 1))
                for b in range(2):
                    pool.wait_ge(s_src, r * 2 + (b + 1))
                    pool.nop(nofuse=True)
                    for j in range(8):
                        pool.indirect_dma_start(source[:, b, j, :], None, tables[LAYERS - 1],
                                                bass.IndirectOffsetOnAxis(src_i[:, b, j:j + 1], 0)).then_inc(s_source[b], 16)
            batch_rows(1, tabs_g[:, 1, :, :])
            batch_rows(2, tabs2_g)

        @block.scalar
        def _(act):
            act.wait_ge(s_records, 1)

            def stage_records(i, h, first):
                if not first:
                    act.wait_ge(s_scat[h], i * (16 * STREAMS))
                act.activation(rec_out[:, h, :, :], rec_s[:, :, bass.ds(i * 2 + h, 1), :].rearrange("p s c f -> p s (c f)"), ACT.Copy)\
                   .then_inc(s_recs[h], 1)
            for h in range(2):
                stage_records(0, h, True)
            with act.Fori(1, SBODIES) as i:
                for h in range(2):
                    stage_records(i, h, False)
            act.wait_ge(s_srt, 16)
            act.wait_ge(s_half, 1)
            half_steps = act.value_load(half_i[0:1, 0:1], min_val=2, max_val=LOOK_BODIES)
            half_less = act.value_load(half_i[0:1, 1:2], min_val=1, max_val=LOOK_BODIES - 1)
            last_set = act.value_load(half_i[0:1, 2:3], min_val=3, max_val=SETS - 1)
            near_last = act.value_load(half_i[0:1, 4:5], min_val=1, max_val=SETS - 3)

            def stage_indices(l, k, h):
                act.wait_ge(s_prod[l][h], k + 1)
                act.nop(nofuse=True)
                step_at = half_steps + k if l == 1 else k
                here = bass.ds(step_at * (2 * HALF) + h * HALF, HALF)
                act.activation(val[:, h, :], srt[:, here, 1], ACT.Copy)
                act.activation(idx[:, h, :], srt[:, here, 2], ACT.Copy).then_inc(s_idx[l][h], 1)

            def turned(q, n):
                for b in range(2):
                    act.wait_ge(s_turned[n][b], q + 2)
                    act.nop(nofuse=True)
                    act.activation(wanted_8[:, b, :], wanted_at[:, bass.ds(q * (2 * HALF) + b * HALF, HALF)], ACT.Copy)
                    act.activation(lookT[:, b, :, :].rearrange("p j e -> p (j e)"), banks[2 + b][:, :].bitcast(f16), ACT.Copy)\
                       .then_inc(s_lookT[n][b], 1)

            def flagged(q, n):
                for b in range(2):
                    act.wait_ge(s_asked[n][b], q + 1)
                    act.nop(nofuse=True)
                    act.activation(flags[:, bass.ds(q * (2 * HALF) + b * HALF, HALF)], banks[4 + b][:, 0:HALF], ACT.Copy)\
                       .then_inc(s_flag[n][b], 1)

            def expand(n_pass):
                act.wait_ge(s_wT, n_pass + 1)
                act.activation(wantedT[:, :, :].rearrange("b c r -> b (c r)"), banks[7][0:BP, :].bitcast(f16)[:, 0:KB * P], ACT.Copy).then_inc(s_wTc, 1)
                for n in range(TS):
                    act.wait_ge(s_expanded, n_pass * TS + n + 1)
                    act.activation(wanted_at[:, n * TW:(n + 1) * TW], banks[5 + n % 2][:, 0:TW], ACT.Copy).then_inc(s_wat, 1)
            expand(0)
            for n in range(2):
                if n == 0:
                    for h in range(2):
                        stage_indices(0, 0, h)
                else:
                    expand(1)
                    act.wait_ge(s_keep, 16)
                stage_indices(n, 1, 0)
                turned(0, n)
                stage_indices(n, 1, 1)
                flagged(0, n)
                turned(1, n)
                with act.Fori(1, half_less) as k:
                    for h in range(2):
                        stage_indices(n, k + 1, h)
                        flagged(k * 2 + (h - 1), n)
                        turned(k * 2 + h, n)
                for h in range(2):
                    if n == 0:
                        act.wait_ge(s_prod[0][h], half_steps + 1)
                        stage_indices(1, 0, h)
                    flagged(near_last + h, n)
                    turned(near_last + (h + 1), n)
                flagged(last_set, n)
            act.wait_ge(s_a_rounds, 2)
            for j in range(MAPCOLS):
                if j:
                    act.wait_ge(s_k_map, j)
                act.activation(k_d, k_c, ACT.Sign, bias=tmap_half[:, j:j + 1], scale=-1.0, accum_out=blk[:, j:j + 1]).then_inc(s_k_map, 1)
            act.wait_ge(s_srt, 32)
            act.wait_ge(s_bodies, 1)
            more = act.value_load(k_bodies_i[0:1, 1:2], min_val=1, max_val=BODIES - 1)
            for h in range(2):
                stage_indices(2, 0, h)
            with act.Fori(0, more) as k:
                for h in range(2):
                    stage_indices(2, k + 1, h)
            for g in range(GROUPS):
                act.wait_ge(s_ft, g + 1)
                if g >= 2:
                    act.wait_ge(s_lm, 2 + g - 1)
                halves = (4, 5) if g % 2 == 0 else (2, 3)
                for i in range(2):
                    act.activation(featT[0:KS, g % 2, 4 * i:4 * i + 4, :].rearrange("k c u -> k (c u)"), banks[halves[i]][0:KS, :], ACT.Copy)
                act.activation(featT[0:DIM, g % 2, KT, :], banks[1 if g % 2 == 0 else 6][0:DIM, 0:P], ACT.Copy).then_inc(s_ftc, 1)

        @block.tensor
        def _(pe):
            pe.wait_ge(s_const, 16)
            for q in range(SLOTS):
                pe.wait_ge(s_mark, q + 1)
                pe.matmul(banks[5][:, 0:BUCKETS], mark_lo[:, q % 2, :], onehot[:, 0, q % 2, :], start=(q == 0), stop=(q == SLOTS - 1))\
                  .then_inc(s_marked, 1)
            HR = HG * HA
            for st in range(STREAMS):
                pe.matmul(banks[st][0:HR, 0:HG * HC], zero_h[:, 0:HR], zero_w[:, 0:HG * HC], start=True, stop=False, skip_group_check=True)
            with pe.Fori(0, HSTEPS) as i:
                for st in range(STREAMS):
                    pe.wait_ge(s_hoh[st], i + 1)
                    for m in range(HM):
                        part = slice(m * HG, (m + 1) * HG)
                        last = pe.matmul(banks[st][0:HR, 0:HG * HC], is_a[:, st, part, :].rearrange("p g a -> p (g a)"),
                                         is_c[:, st, part, :].rearrange("p g c -> p (g c)"), start=False, stop=False, skip_group_check=True)
                    last.then_inc(s_hused[st], 1)
            pe.wait_ge(s_ones, 1)
            for st in range(STREAMS):
                pe.wait_ge(s_hspread, st + 1)
                pe.matmul(banks[st][:, 0:HA * HC], ones_f[0:HR, :], spread_c[0:HR, st % 2, :, :].rearrange("p a c -> p (a c)"), start=True, stop=True)\
                  .then_inc(s_counted, 1)
            pe.wait_ge(s_base, 1)
            for s in range(STREAMS):
                pe.matmul(count[s], ident[:, :], base[:, s, :], start=True, stop=False, skip_group_check=True)
            with pe.Fori(0, SBODIES) as i:
                for h in range(2):
                    pe.wait_ge(s_roh[h], i + 1)
                    for s in range(STREAMS):
                        pe.matmul(count[s], below[:, :], onehot[:, h, s, :], start=False, stop=False, skip_group_check=True)\
                          .then_inc(s_rank[h], 1)
                    for s in range(STREAMS):
                        pe.wait_ge(s_read[h], i * STREAMS + s + 1)
                        last = pe.matmul(count[s], rest[:, :], onehot[:, h, s, :], start=False, stop=False, skip_group_check=True)
                    last.then_inc(s_rused[h], 1)
            zeros_h = zero_w[:, :]

            pe.wait_ge(s_half, 1)
            half_steps = pe.value_load(half_i[0:1, 0:1], min_val=2, max_val=LOOK_BODIES)
            last_set = pe.value_load(half_i[0:1, 2:3], min_val=3, max_val=SETS - 1)

            def products(l, k, h):
                step_at = half_steps + k if l == 1 else k
                _, at = nc.values_load_multi_w_load_instructions(
                    ahead[0:1, bass.ds(step_at * (2 * HALF) + h * HALF, HALF)],
                    engines=[mybir.EngineType.PE], min_val=0, max_val=(HALF - 1) * DIM)
                pe.wait_ge(s_sel[l][h], k + 1)
                pe.wait_ge(s_add[l], k * 2 + (h + CREDIT - 1))
                pe.wait_ge(s_got[l][h], k * (16 * HALF) + 16 * HALF)
                pe.matmul(banks[h][:, :], zero_h[:, :], zeros_h, start=True, stop=False, skip_group_check=True)
                for j in range(HALF):
                    last = pe.matmul(banks[h][:, bass.ds(at[j], DIM)], sel[:, h, j, :], got[:, h, j, :], start=False, stop=(j == HALF - 1), skip_group_check=True)
                last.then_inc(s_prod[l][h], 1)

            def turn_over(q, n):
                for b in range(2):
                    pe.wait_ge(s_look[n][b], q + 1)
                    for j in range(HALF):
                        last = pe.transpose(banks[2 + b][:, :].bitcast(f16)[:, j * P:(j + 1) * P], look[:, b, j, :], ident_h[:, :])
                    last.then_inc(s_turned[n][b], 1)

            def ask(q, n):
                for b in range(2):
                    pe.wait_ge(s_lookT[n][b], q + 1)
                    pe.wait_ge(s_flag[n][b], q + 1)
                    for j in range(HALF):
                        last = pe.matmul(banks[4 + b][:, j:j + 1], lookT[:, b, j, :], wanted_8[:, b, j:j + 1], start=True, stop=True)
                    last.then_inc(s_asked[n][b], 1)

            def expand(n_pass, ones_of):
                pe.wait_ge(s_wanted, n_pass + 1)
                for c in range(KB):
                    last = pe.transpose(banks[7][0:BP, :].bitcast(f16)[:, c * P:(c + 1) * P], wanted[:, c * BP:(c + 1) * BP], ident_h[:, :])
                last.then_inc(s_wT, 1)
                pe.wait_ge(s_wTc, n_pass + 1)
                for n in range(TS):
                    pe.wait_ge(s_expand, n_pass * TS + n + 1)
                    if n >= 2:
                        pe.wait_ge(s_wat, n_pass * TS + n - 1)
                    for c in range(KB):
                        last = pe.matmul(banks[5 + n % 2][:, 0:TW], wantedT[:, c, :], ones_of[0:BP, n % 2, c, :], start=(c == 0), stop=(c == KB - 1))
                    last.then_inc(s_expanded, 1)
                pe.wait_ge(s_wat, (n_pass + 1) * TS)

            expand(0, bucket_is)
            pe.wait_ge(s_windows, 1)
            for n in range(2):
                for h in range(2):
                    pe.sem_inc(s_turned[n][h], 1)
                    pe.sem_inc(s_flag[n][h], 1)
                if n == 0:
                    for h in range(2):
                        pe.sem_inc(s_prod[0][h], 1)
                        pe.sem_inc(s_prod[1][h], 1)
                else:
                    pe.wait_ge(s_a_near, 1)
                    pe.transpose(banks[6][0:1, 0:P], a_near, ident[:, :]).then_inc(s_a_nearT, 1)
                    pe.matmul(banks[7][:, 0:BUCKETS], ident_h[:, :], wanted[:, :], start=True, stop=False, skip_group_check=True)
                    pe.wait_ge(s_a_rounds, 1)
                    turns = pe.value_load(a_rounds_i[0:1, 0:1], min_val=1, max_val=CHUNKS // 8)
                    with pe.Fori(0, turns) as r:
                        pe.wait_ge(s_a_mark, r + 1)
                        for j in range(8):
                            last = pe.matmul(banks[7][:, 0:BUCKETS], a_lo[:, j, :], a_hi[:, j, :], start=False, stop=False, skip_group_check=True)
                        last.then_inc(s_a_marked, 1)
                    expand(1, a_bucket_is)
                products(n, 0, 0)
                turn_over(0, n)
                products(n, 0, 1)
                ask(0, n)
                turn_over(1, n)
                with pe.Fori(1, half_steps) as k:
                    for h in range(2):
                        products(n, k, h)
                        ask(k * 2 + (h - 1), n)
                        turn_over(k * 2 + h, n)
                ask(last_set, n)
            pe.wait_ge(s_a_near, 6)
            pe.transpose(banks[6][0:1, 0:P], k_near, ident[:, :]).then_inc(s_a_nearT, 1)
            for n in range(TS):
                if n >= 2:
                    pe.wait_ge(s_k_read, n - 1)
                pe.matmul(banks[2 + n % 2][:, 0:TW], ones[:, :], flags[:, n * TW:(n + 1) * TW], start=True, stop=True)
                pe.matmul(banks[4 + n % 2][:, 0:TW], rest[:, :], flags[:, n * TW:(n + 1) * TW], start=True, stop=True).then_inc(s_k_sums, 1)
            pe.wait_ge(s_windows, 2)
            pe.wait_ge(s_bodies, 1)
            steps2 = pe.value_load(k_bodies_i[0:1, 0:1], min_val=2, max_val=BODIES)
            for h in range(2):
                pe.sem_inc(s_prod[2][h], 1)
            with pe.Fori(0, steps2) as k:
                for h in range(2):
                    products(2, k, h)
            pe.wait_ge(s_a_near, 11)
            pe.transpose(banks[7][0:1, 0:P], near, ident[:, :]).then_inc(s_a_nearT, 1)
            pe.wait_ge(s_lmw, 32)
            for c in range(KT):
                last = pe.transpose(banks[2][0:KS, c * DIM:(c + 1) * DIM], phi4_sb[:, c * KS:(c + 1) * KS], ident[0:DIM, 0:DIM])
            last.then_inc(s_lm, 1)
            pe.wait_ge(s_lmc, 1)
            for c in range(KT):
                last = pe.matmul(banks[3][0:DIM, 0:DIM], phi4T[:, c, :], ulm[:, c, :], start=(c == 0), stop=(c == KT - 1))
            last.then_inc(s_lm, 1)
            pe.wait_ge(s_lmg, 16 * 3 * GROUPS)
            pe.wait_ge(s_lmc, 3)

            def features(g):
                halves = (4, 5) if g % 2 == 0 else (2, 3)
                if g >= 2:
                    pe.wait_ge(s_ftc, g - 1)
                for c in range(KT):
                    pe.transpose(banks[halves[c // 4]][0:KS, c % 4 * P:(c % 4 + 1) * P], phi2_g[:, g, c * KS:(c + 1) * KS], ident[:, :])
                pe.transpose(banks[1 if g % 2 == 0 else 6][0:DIM, 0:P], phi3_g[:, g, :], ident[:, :]).then_inc(s_ft, 1)
            features(0)
            features(1)
            for g in range(GROUPS):
                pe.wait_ge(s_ftc, g + 1)
                for c in range(KT):
                    pe.matmul(banks[0][:, g * DIM:(g + 1) * DIM], featT[0:KS, g % 2, c, :], ulm9[:, c, :], start=(c == 0), stop=False, skip_group_check=True)
                pe.matmul(banks[0][:, g * DIM:(g + 1) * DIM], featT[0:DIM, g % 2, KT, :], w1[:, :], start=False, stop=True, skip_group_check=True)\
                  .then_inc(s_lm, 1)
                if g + 2 < GROUPS:
                    features(g + 2)
            pe.wait_ge(s_a_rounds, 3)
            turns = pe.value_load(rounds_i[0:1, 0:1], min_val=1, max_val=CHUNKS // 8)
            for b in range(2):
                pe.matmul(banks[6 + b][:, :], zero_h[:, :], zero_w[:, :], start=True, stop=False, skip_group_check=True)

            for i in range(2):
                pe.sem_inc(s_matched[i], 1)

            def spread(r, b):
                pe.wait_ge(s_split, r * 12 + (b * 6 + 6))
                for j in range(8):
                    pe.wait_ge(s_match[j % 2], r * 8 + (b * 4 + j // 2 + 1))
                    for q, part in ((q, part) for q in range(SLOTS) for part in range(3)):
                        last = pe.matmul(banks[6 + q // GROUPS][:, (q % GROUPS) * DIM:(q % GROUPS + 1) * DIM],
                                         match[:, j % 2, q * P:(q + 1) * P], parts[:, part, b * 8 + j, :], start=False, stop=False, skip_group_check=True)
                    last.then_inc(s_matched[j % 2], 1)
            with pe.Fori(0, turns) as r:
                for b in range(2):
                    spread(r, b)

        @block.vector
        def _(dve):
            steps = [0]

            def step(ins):
                steps[0] += 1
                ins.then_inc(s_prep, 1)
                dve.wait_ge(s_prep, steps[0])

            dve.memset(raw_rows[:, FULL:COLS], BLOCKS * P).then_inc(s_tail, 1)
            dve.memset(raw_cols[:, FULL:COLS], 0).then_inc(s_tail, 1)
            dve.memset(raw_vals[:, FULL:COLS], 0.0).then_inc(s_tail, 1)
            dve.memset(srt[:, :, :], 0.0).then_inc(s_vconst, 1)
            dve.memset(zero_b[:, :], 0.0).then_inc(s_vconst, 1)
            dve.memset(flags[:, :], 0.0).then_inc(s_vconst, 1)
            dve.wait_ge(s_batch, 32)
            for side, size in ((0, N_USERS), (1, N_ITEMS)):
                step(dve.tensor_copy(r_f[:, side, :], r_i[:, side, :]))
                step(dve.tensor_scalar(r_neg[:, side, :], r_f[:, side, :], 0.0, float(size), ALU.is_lt, ALU.mult))
                step(dve.tensor_tensor(r_c[:, side, :], r_f[:, side, :], r_neg[:, side, :], ALU.add))
                step(dve.tensor_scalar(r_f[:, side, :], r_c[:, side, :], 0.0, float(size - 1), ALU.max, ALU.min))
                step(dve.tensor_copy(r_idx[:, side, :], r_f[:, side, :]))
                step(dve.tensor_scalar(n_f[:, side, :], r_f[:, side, :], float(N_USERS * side), None, ALU.add))
                step(dve.tensor_copy(n_i[:, side, :], n_f[:, side, :]))
            step(dve.tensor_scalar(n_lo[:, :, :], n_i[:, :, :], P - 1, None, ALU.bitwise_and))
            step(dve.tensor_scalar(n_hi[:, :, :], n_i[:, :, :], 7, None, ALU.arith_shift_right))
            step(dve.scalar_tensor_tensor(t_idx[:, :, :], n_lo[:, :, :], float(BUCKETS), n_hi[:, :, :], ALU.mult, ALU.add))
            step(dve.tensor_copy(n_lo_f[:, :, :], n_lo[:, :, :]))
            step(dve.tensor_copy(n_hi_f[:, :, :], n_hi[:, :, :]))
            dve.sem_inc(s_nf, 1)
            dve.wait_ge(s_const, 16)
            step(dve.tensor_copy(iota_b[:, :], iota_i[:, :]))
            step(dve.tensor_copy(iota_r[:, :], iota_i[:, 0:P]))
            step(dve.tensor_copy(tmap[:, :], tmap_i[:, :]))
            step(dve.tensor_scalar(tmap_half[:, :], tmap[:, :], 0.5, None, ALU.add))
            step(dve.tensor_copy(row_base[:, :], row_base_i[:, :]))
            step(dve.tensor_copy(part_node[:, :], part_node_i[:, :]))
            step(dve.tensor_copy(ident_h[:, :], ident[:, :]))
            for q in range(SLOTS):
                side, g = q // GROUPS, q % GROUPS
                if q >= 2:
                    dve.wait_ge(s_marked, q - 1)
                dve.tensor_scalar(mark_lo[:, q % 2, :], iota_b[:, 0:P], n_lo_f[:, side, g:g + 1], None, ALU.is_equal)
                dve.tensor_scalar(onehot[:, 0, q % 2, :], iota_b[:, :], n_hi_f[:, side, g:g + 1], None, ALU.is_equal).then_inc(s_mark, 1)
            dve.wait_ge(s_marked, SLOTS)
            step(dve.tensor_scalar(wanted[:, :], banks[5][:, 0:BUCKETS], 0.0, None, ALU.is_gt))
            dve.sem_inc(s_wanted, 1)
            dve.wait_ge(s_load, 96)
            step(dve.tensor_scalar(scratch_i, raw_rows, 7, None, ALU.arith_shift_right))
            step(dve.tensor_copy(hi, scratch_i))

            def one_hots(i, h, into):
                for s in range(STREAMS):
                    last = dve.tensor_scalar(onehot[:, h, s, :], iota_b[:, :], hi[:, bass.ds(i * 2 + (h + s * SCOLS), 1)], None, ALU.is_equal)
                last.then_inc(into[h], 1)

            step(dve.tensor_scalar(scratch_i, raw_rows, 7 + HC.bit_length() - 1, None, ALU.arith_shift_right))
            step(dve.tensor_copy(hi_a, scratch_i))
            step(dve.tensor_scalar(scratch_i, raw_rows, 7, HC - 1, ALU.arith_shift_right, ALU.bitwise_and))
            step(dve.tensor_copy(hi_c, scratch_i))
            step(dve.memset(ones_f[:, :], 1.0))
            step(dve.tensor_reduce(own_a[:, :], own_as[:, :, :], AX.X, ALU.add))
            dve.sem_inc(s_ones, 1)

            def histogram(i, st):
                here = bass.ds(i * HCOLS + st * SCOLS, HCOLS)
                for out_, values, n in ((is_a, hi_a, HA), (is_c, hi_c, HC)):
                    last = dve.tensor_tensor(out_[:, st, :, :], iota_b[:, 0:n].unsqueeze(1).to_broadcast([P, HCOLS, n]),
                                             values[:, here].unsqueeze(2).to_broadcast([P, HCOLS, n]), ALU.is_equal)
                last.then_inc(s_hoh[st], 1)
            for st in range(STREAMS):
                histogram(0, st)
            with dve.Fori(1, HSTEPS) as i:
                for st in range(STREAMS):
                    dve.wait_ge(s_hused[st], i)
                    histogram(i, st)
            step(dve.tensor_copy(rec[:, :, 0], raw_rows))
            step(dve.tensor_scalar(scratch_i, raw_cols, P - 1, None, ALU.bitwise_and))
            step(dve.tensor_scalar(raw_rows, raw_cols, 7, None, ALU.arith_shift_right))
            step(dve.scalar_tensor_tensor(rec[:, :, 2], scratch_i, float(BUCKETS), raw_rows, ALU.mult, ALU.add))
            step(dve.tensor_copy(rec[:, :, 1], raw_vals))
            dve.sem_inc(s_records, 1)
            HR = HG * HA
            for st in range(STREAMS):
                dve.wait_ge(s_hused[st], HSTEPS)
                dve.tensor_tensor(folded[0:HR, st, :, :], banks[st][0:HR, 0:HG * HC].rearrange("p (g c) -> p g c", c=HC), own_group[0:HR, :, :], ALU.mult)\
                   .then_inc(s_hfold, 1)
                dve.wait_ge(s_hfold, 2 * st + 1)
                dve.tensor_reduce(part_of[0:HR, st, :], folded[0:HR, st, :, :].rearrange("p g c -> p c g"), AX.X, ALU.add).then_inc(s_hfold, 1)
                dve.wait_ge(s_hfold, 2 * st + 2)
                if st >= 2:
                    dve.wait_ge(s_counted, st - 1)
                dve.tensor_tensor(spread_c[0:HR, st % 2, :, :], part_of[0:HR, st, :].unsqueeze(1).to_broadcast([HR, HA, HC]),
                                  own_a[0:HR, :].unsqueeze(2).to_broadcast([HR, HA, HC]), ALU.mult).then_inc(s_hspread, 1)
            dve.wait_ge(s_counted, STREAMS)
            step(dve.tensor_copy(base[:, 1, :], count[0]))
            for s in range(1, STREAMS):
                step(dve.tensor_tensor(base[:, s + 1, :], base[:, s, :], count[s], ALU.add))
            step(dve.tensor_scalar(cnt_i[:, :], base[:, STREAMS, :], float(P - 1), None, ALU.add))
            step(dve.tensor_scalar(nch_i[:, :], cnt_i[:, :], 7, None, ALU.arith_shift_right))
            step(dve.tensor_scalar(nch[:, :], nch_i[:, :], 1.0, None, ALU.max))
            step(dve.tensor_tensor_scan(ends[:, :], nch[:, :], zero_b[:, :], 0.0, ALU.add, ALU.add))
            step(dve.tensor_tensor(cnt[:, :], ends[:, :], nch[:, :], ALU.subtract))
            step(dve.tensor_scalar(base[:, 0, :], cnt[:, :], float(P), None, ALU.mult))
            for s in range(1, STREAMS):
                step(dve.tensor_tensor(base[:, s, :], base[:, s, :], base[:, 0, :], ALU.add))
            dve.sem_inc(s_base, 1)
            step(dve.tensor_scalar(half_f[0:1, 0:1], cnt[0:1, BUCKETS - 1:BUCKETS], float(4 * HALF - 1), None, ALU.add))
            step(dve.tensor_copy(half_i[0:1, 3:4], half_f[0:1, 0:1]))
            step(dve.tensor_scalar(half_i[0:1, 0:1], half_i[0:1, 3:4], (4 * HALF).bit_length() - 1, None, ALU.arith_shift_right))
            step(dve.tensor_copy(half_f[0:1, 1:2], half_i[0:1, 0:1]))
            step(dve.tensor_scalar(half_i[0:1, 1:2], half_f[0:1, 1:2], -1.0, None, ALU.add))
            step(dve.tensor_scalar(half_i[0:1, 2:3], half_f[0:1, 1:2], 2.0, -1.0, ALU.mult, ALU.add))
            step(dve.tensor_scalar(half_i[0:1, 4:5], half_f[0:1, 1:2], 2.0, -3.0, ALU.mult, ALU.add))
            step(dve.tensor_scalar(half_i[0:1, 3:4], half_f[0:1, 1:2], 2.0, None, ALU.mult))
            dve.sem_inc(s_half, 1)
            for j in range(MAPCOLS):
                step(dve.tensor_scalar(picked[:, :], ends[:, :], tmap[:, j:j + 1], 0.0, ALU.is_le, ALU.add, accum_out=blk[:, j:j + 1]))
            step(dve.tensor_scalar(first_16[:, :], blk[:, :], float(BUCKETS - 1), float(P), ALU.min, ALU.mult))
            dve.sem_inc(s_mapo, 1)


            def places(i, h, first, nth):
                for s in range(STREAMS):
                    dve.wait_ge(s_rank[h], i * STREAMS + s + 1)
                    if s:
                        dve.wait_ge(s_read[h], i * STREAMS + s)
                    dve.scalar_tensor_tensor(picked[:, :], iota_b[:, :], hi[:, bass.ds(i * 2 + (h + s * SCOLS), 1)], count[s],
                                             ALU.is_equal, ALU.mult, accum_out=pos[:, h, s:s + 1]).then_inc(s_read[h], 1)
                dve.wait_ge(s_read[h], i * STREAMS + STREAMS)
                dve.tensor_copy(pos_i[:, h, :], pos[:, h, :]).then_inc(s_pc, 1)
                dve.wait_ge(s_pc, nth * 3 + 1)
                dve.tensor_scalar(pos_lo[:, h, :], pos_i[:, h, :], P - 1, None, ALU.bitwise_and).then_inc(s_pc, 1)
                dve.tensor_scalar(pos_hi[:, h, :], pos_i[:, h, :], 7, None, ALU.arith_shift_right).then_inc(s_pc, 1)
                dve.wait_ge(s_pc, nth * 3 + 3)
                if not first:
                    dve.wait_ge(s_scat[h], i * (16 * STREAMS))
                dve.scalar_tensor_tensor(pos_out[:, h, :], pos_lo[:, h, :], float(CHUNKS), pos_hi[:, h, :], ALU.mult, ALU.add)\
                   .then_inc(s_pos[h], 1)

            for st in range(STREAMS):
                dve.wait_ge(s_hused[st], HSTEPS)
            one_hots(0, 0, s_roh)
            one_hots(0, 1, s_roh)
            places(0, 0, True, 0)
            dve.wait_ge(s_rused[0], 1)
            one_hots(1, 0, s_roh)
            places(0, 1, True, 1)
            dve.wait_ge(s_rused[1], 1)
            one_hots(1, 1, s_roh)
            places(1, 0, False, 2)
            with dve.Fori(2, SBODIES) as i:
                dve.wait_ge(s_rused[0], i)
                one_hots(i, 0, s_roh)
                places(i - 1, 1, False, i * 2 - 1)
                dve.wait_ge(s_rused[1], i)
                one_hots(i, 1, s_roh)
                places(i, 0, False, i * 2)
            places(SBODIES - 1, 1, False, 2 * SBODIES - 1)

            def selectors(l, k, h):
                dve.wait_ge(s_prod[l][h], k + 1)
                step_at = half_steps + k if l == 1 else k
                here = bass.ds(step_at * (2 * HALF) + h * HALF, HALF)
                dve.tensor_tensor(low[:, h, :], srt[:, here, 0], first[:, here], ALU.subtract).then_inc(s_low[l], 1)
                dve.wait_ge(s_idx[l][h], k + 1)
                dve.wait_ge(s_low[l], k * 2 + (h + 1))
                for j in range(HALF):
                    last = dve.tensor_scalar(sel[:, h, j, :], iota_r[:, :], low[:, h, j:j + 1], val[:, h, j:j + 1], ALU.is_equal, ALU.mult)
                last.then_inc(s_sel[l][h], 1)

            def add_products(l, k, h):
                step_at = half_steps + k if l == 1 else k
                at = dve.value_load(window[0:1, bass.ds(step_at * 2 + h, 1)], min_val=0, max_val=(BUCKETS - 1) * DIM)
                dve.wait_ge(s_prod[l][h], k + 2)
                dve.wait_ge(s_add[l], k * 2 + (h + CREDIT))
                dst = acc[:, bass.ds(at, HALF * DIM)]
                dve.tensor_tensor(dst, dst, banks[h][:, :], ALU.add).then_inc(s_add[l], 1)
                dve.wait_ge(s_add[l], k * 2 + (h + 1 + CREDIT))

            def look_up(q, n=0):
                for b in range(2):
                    here = bass.ds(q * (2 * HALF) + b * HALF, HALF)
                    dve.wait_ge(s_turned[n][b], q + 1)
                    dve.tensor_tensor(look_low[:, b, :], srt[:, here, 0], first[:, here], ALU.subtract).then_inc(s_llow[n], 1)
                    dve.wait_ge(s_llow[n], q * 2 + (b + 1))
                    for j in range(HALF):
                        last = dve.tensor_scalar(look[:, b, j, :], iota_b[:, 0:P], look_low[:, b, j:j + 1], None, ALU.is_equal)
                    last.then_inc(s_look[n][b], 1)

            half_steps = dve.value_load(half_i[0:1, 0:1], min_val=2, max_val=LOOK_BODIES)
            half_less = dve.value_load(half_i[0:1, 1:2], min_val=1, max_val=LOOK_BODIES - 1)
            last_set = dve.value_load(half_i[0:1, 2:3], min_val=3, max_val=SETS - 1)
            def windows():
                by_half = first[0:1, :].rearrange("p (n j) -> p n j", j=HALF)
                step(dve.tensor_tensor(first_d[0:1, :].rearrange("p (n j) -> p n j", j=HALF), by_half,
                                        by_half[:, :, 0:1].to_broadcast([1, CHUNKS // HALF, HALF]), ALU.subtract))
                step(dve.tensor_scalar(ahead[:, :], first_d[0:1, :], DIM / P, None, ALU.mult))
                step(dve.tensor_scalar(window[:, :], by_half[:, :, 0], DIM / P, None, ALU.mult))
                dve.sem_inc(s_windows, 1)

            def expand(n_pass, ones_of):
                for n in range(TS):
                    if n >= 2:
                        dve.wait_ge(s_expanded, n_pass * TS + n - 1)
                    for c in range(KB):
                        last = dve.tensor_scalar(ones_of[0:BP, n % 2, c, :], first[0:BP, n * TW:(n + 1) * TW], part_node[0:BP, c:c + 1], None, ALU.is_equal)
                    last.then_inc(s_expand, 1)
                dve.wait_ge(s_expanded, (n_pass + 1) * TS)

            def count_rounds(n, bank, rounds_f_, rounds_i_, per, shift):
                dve.wait_ge(s_a_nearT, n + 1)
                dve.tensor_reduce(rounds_f_[0:1, 0:1], banks[bank][0:1, 0:P], AX.X, ALU.max).then_inc(s_a_near, 1)
                dve.wait_ge(s_a_near, 5 * n + 2)
                dve.tensor_scalar(rounds_f_[0:1, 1:2], rounds_f_[0:1, 0:1], float(per - 1), float(per), ALU.add, ALU.max).then_inc(s_a_near, 1)
                dve.wait_ge(s_a_near, 5 * n + 3)
                dve.tensor_copy(rounds_i_[0:1, 1:2], rounds_f_[0:1, 1:2]).then_inc(s_a_near, 1)
                dve.wait_ge(s_a_near, 5 * n + 4)
                dve.tensor_scalar(rounds_i_[0:1, 0:1], rounds_i_[0:1, 1:2], shift, None, ALU.arith_shift_right).then_inc(s_a_near, 1)
                dve.wait_ge(s_a_near, 5 * n + 5)

            dve.wait_ge(s_srt, 16)
            dve.wait_ge(s_map, 32)
            windows()
            for h in range(2):
                dve.wait_ge(s_rused[h], SBODIES)
            expand(0, bucket_is)
            dve.memset(acc[:, :], 0.0).then_inc(s_zacc, 1)
            dve.wait_ge(s_zacc, 1)
            for l in range(STAGES):
                dve.sem_inc(s_add[l], CREDIT)
            selectors(0, 0, 0)
            selectors(0, 0, 1)
            look_up(0, 0)
            with dve.Fori(0, half_less) as k:
                for h in range(2):
                    add_products(0, k, h)
                    selectors(0, k + 1, h)
                    look_up(k * 2 + (h + 1), 0)
            for h in range(2):
                add_products(0, half_less, h)
                selectors(1, 0, h)
                if h == 0:
                    look_up(last_set, 0)

            for b in range(2):
                dve.wait_ge(s_flag[0][b], last_set + 2)
            dve.tensor_reduce(a_near, flags[:, :], AX.X, ALU.add).then_inc(s_a_near, 1)
            count_rounds(0, 6, a_rounds_f, a_rounds_i, 8, 3)
            dve.sem_inc(s_a_rounds, 1)
            turns = dve.value_load(a_rounds_i[0:1, 0:1], min_val=1, max_val=CHUNKS // 8)
            dve.wait_ge(s_k_const, 1)
            step(dve.tensor_copy(a_steps, a_step_i))
            step(dve.memset(a_keys, 1.0))
            step(dve.tensor_tensor_scan(a_keys, a_keys, zero_b[:, 0:1].to_broadcast([P, CHUNKS]), 0.0, ALU.add, ALU.add))
            step(dve.tensor_scalar(a_keys, a_keys, -1.0, float(CHUNKS + 1), ALU.mult, ALU.add))
            step(dve.tensor_tensor(a_keys, a_keys, flags[:, :], ALU.mult))
            with dve.Fori(0, turns) as r:
                STEPS = 15
                dve.nop(nofuse=True)
                dve.max(a_top, a_keys).then_inc(s_a_pick, 1)
                dve.wait_ge(s_a_pick, r * STEPS + 1)
                dve.scalar_tensor_tensor(a_keys, a_keys, a_top[:, 7:8], a_keys, ALU.is_lt, ALU.mult).then_inc(s_a_pick, 1)
                dve.tensor_scalar(a_valid, a_top, 0.0, None, ALU.is_gt).then_inc(s_a_pick, 1)
                dve.tensor_scalar(a_at_f, a_top, -1.0, float(CHUNKS), ALU.mult, ALU.add).then_inc(s_a_pick, 1)
                dve.wait_ge(s_a_pick, r * STEPS + 4)
                dve.tensor_scalar(a_at_i, a_at_f, float(CHUNKS - 1), row_base[:, :], ALU.min, ALU.add).then_inc(s_a_at, 1)
                dve.wait_ge(s_a_found, r * (16 * 8) + 16 * 8)
                dve.scalar_tensor_tensor(a_tab, a_found[:, :, 2], 1.0, a_valid, ALU.add, ALU.mult).then_inc(s_a_pick, 1)
                dve.wait_ge(s_a_pick, r * STEPS + 5)
                for j in range(8):
                    if j:
                        dve.wait_ge(s_a_pick, r * STEPS + (5 + j))
                    dve.tensor_scalar(a_le, a_steps, a_tab[:, j:j + 1], 0.0, ALU.is_le, ALU.add, accum_out=a_lo_n[:, j:j + 1]).then_inc(s_a_pick, 1)
                dve.wait_ge(s_a_pick, r * STEPS + 13)
                dve.tensor_scalar(a_lo_m, a_lo_n, -float(BUCKETS), float(BUCKETS - 1), ALU.mult, ALU.add).then_inc(s_a_pick, 1)
                dve.wait_ge(s_a_pick, r * STEPS + 14)
                dve.tensor_tensor(a_hi_n, a_lo_m, a_tab, ALU.add).then_inc(s_a_pick, 1)
                dve.tensor_scalar(a_at_f, a_lo_n, -1.0, None, ALU.add).then_inc(s_a_lo, 1)
                dve.wait_ge(s_a_pick, r * STEPS + 15)
                dve.wait_ge(s_a_lo, r + 1)
                for j in range(8):
                    dve.tensor_scalar(a_lo[:, j, :], iota_b[:, 0:P], a_at_f[:, j:j + 1], None, ALU.is_equal)
                    last = dve.tensor_scalar(a_hi[:, j, :], iota_b[:, :], a_hi_n[:, j:j + 1], None, ALU.is_equal)
                last.then_inc(s_a_mark, 1)
                dve.wait_ge(s_a_marked, r + 1)
            step(dve.tensor_scalar(wanted[:, :], banks[7][:, 0:BUCKETS], 0.0, None, ALU.is_gt))
            dve.sem_inc(s_wanted, 1)
            expand(1, a_bucket_is)
            look_up(0, 1)
            with dve.Fori(0, half_less) as k:
                for h in range(2):
                    add_products(1, k, h)
                    selectors(1, k + 1, h)
                    look_up(k * 2 + (h + 1), 1)
            for h in range(2):
                add_products(1, half_less, h)
                if h == 0:
                    look_up(last_set, 1)
            dve.sem_inc(s_layer, 1)

            for b in range(2):
                dve.wait_ge(s_flag[1][b], last_set + 2)
            dve.tensor_reduce(k_near, flags[:, :], AX.X, ALU.add).then_inc(s_a_near, 1)
            count_rounds(1, 6, k_rounds_f, k_rounds_i, 16, 4)
            for n in range(TS):
                dve.wait_ge(s_k_sums, n + 1)
                dve.tensor_copy(k_col[:, n * TW:(n + 1) * TW], banks[2 + n % 2][:, 0:TW])
                dve.tensor_copy(k_rank[:, n * TW:(n + 1) * TW], banks[4 + n % 2][:, 0:TW]).then_inc(s_k_read, 1)
            dve.wait_ge(s_k_read, TS)
            step(dve.memset(k_same[:, 0:1], 0.0))
            step(dve.tensor_tensor(k_same[:, 1:CHUNKS], first[:, 1:CHUNKS], first[:, 0:CHUNKS - 1], ALU.is_equal))
            step(dve.tensor_tensor_scan(k_c, k_same, k_col, 0.0, ALU.mult, ALU.add))
            step(dve.scalar_tensor_tensor(k_rank, k_rank, float(P * CHUNKS), k_c, ALU.add, ALU.subtract))
            step(dve.memset(k_col[:, CHUNKS - 1:CHUNKS], 1.0))
            step(dve.tensor_scalar(k_col[:, 0:CHUNKS - 1], k_same[:, 1:CHUNKS], -1.0, 1.0, ALU.mult, ALU.add))
            step(dve.tensor_scalar(k_d.bitcast(i32), k_c, float(P - 1), None, ALU.add))
            step(dve.tensor_scalar(k_c.bitcast(i32), k_d.bitcast(i32), 7, None, ALU.arith_shift_right))
            step(dve.scalar_tensor_tensor(k_d, k_c.bitcast(i32), 1.0, k_col, ALU.max, ALU.mult))
            step(dve.tensor_tensor_scan(k_c, k_d, zero_b[:, 0:1].to_broadcast([P, CHUNKS]), 0.0, ALU.add, ALU.add))
            step(dve.tensor_tensor(k_d, k_c, k_d, ALU.subtract))
            step(dve.scalar_tensor_tensor(k_rank, k_d, -float(P), k_rank, ALU.mult, ALU.add))
            step(dve.tensor_tensor(k_rank, k_rank, flags[:, :], ALU.mult))
            FAR = float(2 ** 20)
            step(dve.scalar_tensor_tensor(k_c[:, 0:CHUNKS - 1], k_same[:, 1:CHUNKS], FAR, k_c[:, 0:CHUNKS - 1], ALU.mult, ALU.add))
            dve.wait_ge(s_k_const, 2)
            step(dve.tensor_copy(k_trash.rearrange("p b j -> p (b j)"), k_trash_i))
            dve.sem_inc(s_a_rounds, 1)
            turns = dve.value_load(k_rounds_i[0:1, 0:1], min_val=1, max_val=CHUNKS // 8)

            def place(r, b):
                STEPS = 11
                at = r * (2 * STEPS) + b * STEPS
                top_ = k_top[:, b, :]
                dve.nop(nofuse=True)
                dve.max(top_, k_rank).then_inc(s_k_pick, 1)
                dve.wait_ge(s_k_pick, at + 1)
                dve.nop(nofuse=True)
                dve.max_index(k_at_u[:, b, :], top_, k_rank).then_inc(s_k_pick, 1)
                dve.wait_ge(s_k_pick, at + 2)
                dve.scalar_tensor_tensor(k_rank, k_rank, top_[:, 7:8], k_rank, ALU.is_lt, ALU.mult).then_inc(s_k_pick, 1)
                dve.tensor_scalar(k_at_f[:, b, :], k_at_u[:, b, :], 0.0, float(CHUNKS - 1), ALU.max, ALU.min).then_inc(s_k_pick, 1)
                dve.tensor_scalar(k_valid[:, b, :], top_, 0.0, None, ALU.is_gt).then_inc(s_k_pick, 1)
                dve.tensor_scalar(k_pos[:, b, :], top_, -1.0, float(P * CHUNKS), ALU.mult, ALU.add).then_inc(s_k_pick, 1)
                dve.wait_ge(s_k_pick, at + 6)
                dve.tensor_scalar(k_lo[:, b, :], k_pos[:, b, :], P - 1, None, ALU.bitwise_and).then_inc(s_k_pick, 1)
                dve.tensor_scalar(k_hi[:, b, :], k_pos[:, b, :], 7, None, ALU.arith_shift_right).then_inc(s_k_pick, 1)
                dve.wait_ge(s_k_pick, at + 8)
                dve.scalar_tensor_tensor(k_row[:, b, :], k_lo[:, b, :], float(CHUNKS), k_hi[:, b, :], ALU.mult, ALU.add).then_inc(s_k_pick, 1)
                dve.wait_ge(s_k_pick, at + 9)
                dve.tensor_tensor(k_row[:, b, :], k_row[:, b, :], k_trash[:, b, :], ALU.subtract).then_inc(s_k_pick, 1)
                dve.wait_ge(s_k_pick, at + 10)
                dve.tensor_tensor(k_row_v[:, b, :], k_row[:, b, :], k_valid[:, b, :], ALU.mult).then_inc(s_k_pick, 1)
                dve.wait_ge(s_k_pick, at + 11)
                dve.wait_ge(s_slot[b], r + 1)
                dve.tensor_scalar(k_at_i[:, b, :], k_at_f[:, b, :], row_base[:, :], None, ALU.add)
                dve.tensor_tensor(k_dst[:, b, :], k_row_v[:, b, :], k_trash[:, b, :], ALU.add).then_inc(s_k_dst, 1)
            with dve.Fori(0, turns) as r:
                for b in range(2):
                    place(r, b)
            step(dve.tensor_scalar(k_bodies_f[0:1, 0:1], k_c[0:1, CHUNKS - 1:CHUNKS], float(2 * HALF - 1), None, ALU.add))
            step(dve.tensor_copy(k_bodies_i[0:1, 2:3], k_bodies_f[0:1, 0:1]))
            step(dve.tensor_scalar(k_bodies_i[0:1, 0:1], k_bodies_i[0:1, 2:3], (2 * HALF).bit_length() - 1, None, ALU.arith_shift_right))
            step(dve.tensor_copy(k_bodies_f[0:1, 1:2], k_bodies_i[0:1, 0:1]))
            step(dve.tensor_scalar(k_bodies_f[0:1, 2:3], k_bodies_f[0:1, 1:2], -1.0, None, ALU.add))
            step(dve.tensor_copy(k_bodies_i[0:1, 1:2], k_bodies_f[0:1, 2:3]))
            dve.sem_inc(s_bodies, 1)
            dve.wait_ge(s_k_map, MAPCOLS)
            step(dve.tensor_scalar(blk[:, :], blk[:, :], 0.5, CHUNKS / 2, ALU.mult, ALU.add))
            step(dve.tensor_scalar(first_16[:, :], blk[:, :], float(BUCKETS - 1), float(P), ALU.min, ALU.mult))
            dve.sem_inc(s_mapo, 1)
            dve.wait_ge(s_tab, 16)
            dve.wait_ge(s_map, 64)
            windows()
            dve.memset(acc[:, :], 0.0).then_inc(s_zacc, 1)
            dve.wait_ge(s_zacc, 2)
            dve.wait_ge(s_srt, 32)
            last_step = dve.value_load(k_bodies_i[0:1, 1:2], min_val=1, max_val=BODIES - 1)
            selectors(2, 0, 0)
            selectors(2, 0, 1)
            with dve.Fori(0, last_step) as k:
                for h in range(2):
                    add_products(2, k, h)
                    selectors(2, k + 1, h)
            for h in range(2):
                add_products(2, last_step, h)
            dve.sem_inc(s_layer, 1)

            dve.wait_ge(s_keep, 32)
            dve.tensor_reduce(near, flags[:, :], AX.X, ALU.add).then_inc(s_a_near, 1)
            count_rounds(2, 7, rounds_f, rounds_i, 16, 4)
            dve.sem_inc(s_a_rounds, 1)
            turns = dve.value_load(rounds_i[0:1, 0:1], min_val=1, max_val=CHUNKS // 8)
            step(dve.memset(keys, 1.0))
            step(dve.tensor_tensor_scan(keys, keys, zero_b[:, 0:1].to_broadcast([P, CHUNKS]), 0.0, ALU.add, ALU.add))
            step(dve.tensor_scalar(keys, keys, -1.0, float(CHUNKS + 1), ALU.mult, ALU.add))
            step(dve.tensor_tensor(keys, keys, flags[:, :], ALU.mult))
            dve.wait_ge(s_lm, 1)
            dve.tensor_copy(phi4T[:, :, :].rearrange("k c d -> k (c d)"), banks[2][0:KS, :]).then_inc(s_lmc, 1)
            dve.wait_ge(s_lm, 2)
            dve.tensor_scalar(w1[:, :], banks[3][0:DIM, 0:DIM], 0.1, None, ALU.mult).then_inc(s_lmc, 1)
            dve.tensor_scalar(ulm9[:, :, :], ulm[:, :, :], 0.9, None, ALU.mult).then_inc(s_lmc, 1)
            STEPS = 5

            def pick(r, b):
                at = r * (2 * STEPS) + b * (STEPS - 1)
                dve.nop(nofuse=True)
                dve.max(top[:, b, :], keys).then_inc(s_top, 1)
                dve.wait_ge(s_top, at + 1)
                dve.scalar_tensor_tensor(keys, keys, top[:, b, 7:8], keys, ALU.is_lt, ALU.mult).then_inc(s_top, 1)
                dve.tensor_scalar(valid[:, b, :], top[:, b, :], 0.0, None, ALU.is_gt).then_inc(s_top, 1)
                dve.tensor_scalar(at_f[:, b, :], top[:, b, :], -1.0, float(CHUNKS), ALU.mult, ALU.add).then_inc(s_top, 1)
                dve.wait_ge(s_top, at + 4)
                dve.tensor_scalar(at_i[:, b, :], at_f[:, b, :], float(CHUNKS - 1), row_base[:, :], ALU.min, ALU.add).then_inc(s_at, 1)

            def read(r, b):
                dve.wait_ge(s_found[b], r * (16 * 8) + 16 * 8)
                dve.tensor_tensor(val8[:, b, :], found[:, b, :, 1], valid[:, b, :], ALU.mult).then_inc(s_top, 1)
                dve.tensor_copy(src_i[:, b, :], found[:, b, :, 2]).then_inc(s_src, 1)
                dve.wait_ge(s_top, r * (2 * STEPS) + (2 * (STEPS - 1) + b + 1))

            def split(r, b):
                dve.wait_ge(s_source[b], r * (16 * 8) + 16 * 8)
                at = r * 12 + b * 6
                part = parts[:, :, b * 8:(b + 1) * 8, :]
                dve.tensor_tensor(left[:, 0, :, :], source[:, b, :, :], val8[:, b, :].unsqueeze(2).to_broadcast([P, 8, DIM]), ALU.mult).then_inc(s_split, 1)
                dve.wait_ge(s_split, at + 1)
                dve.tensor_copy(part[:, 0, :, :], left[:, 0, :, :]).then_inc(s_split, 1)
                dve.wait_ge(s_split, at + 2)
                dve.tensor_tensor(left[:, 1, :, :], left[:, 0, :, :], part[:, 0, :, :], ALU.subtract).then_inc(s_split, 1)
                dve.wait_ge(s_split, at + 3)
                dve.tensor_copy(part[:, 1, :, :], left[:, 1, :, :]).then_inc(s_split, 1)
                dve.wait_ge(s_split, at + 4)
                dve.tensor_tensor(left[:, 0, :, :], left[:, 1, :, :], part[:, 1, :, :], ALU.subtract).then_inc(s_split, 1)
                dve.wait_ge(s_split, at + 5)
                dve.tensor_copy(part[:, 2, :, :], left[:, 0, :, :]).then_inc(s_split, 1)

            def compare(r, b):
                for j in range(8):
                    dve.wait_ge(s_matched[j % 2], r * 8 + (b * 4 + j // 2 + 1))
                    dve.tensor_scalar(match[:, j % 2, :].rearrange("p (q u) -> p q u", q=SLOTS), nodes, found[:, b, j, 0:1], None,
                                      ALU.is_equal).then_inc(s_match[j % 2], 1)
            with dve.Fori(0, turns) as r:
                for b in range(2):
                    pick(r, b)
                for b in range(2):
                    read(r, b)
                dve.wait_ge(s_nodes, 32)
                for b in range(2):
                    split(r, b)
                    compare(r, b)
                for i in range(2):
                    dve.wait_ge(s_matched[i], r * 8 + 9)

            dve.wait_ge(s_lm, 2 + GROUPS)
            dve.tensor_tensor(user_lm[:, :, :].rearrange("p g d -> p (g d)"), banks[0][:, :],
                              ilm_g[:, :, :].rearrange("p g d -> p (g d)"), ALU.mult).then_inc(s_lmc, 1)
            dve.wait_ge(s_lmc, 4)
            dve.tensor_reduce(gamma_lm[:, :], user_lm[:, :, :], AX.X, ALU.add).then_inc(s_lmc, 1)
            dve.wait_ge(s_light, 16 * SLOTS * LAYERS)
            dve.tensor_reduce(light[:, :, :].rearrange("p n d -> p (n d)"), tabs_g.rearrange("p l n d -> p (n d) l"), AX.X, ALU.add).then_inc(s_fold, 1)
            dve.wait_ge(s_fold, 1)
            dve.tensor_tensor(light[:, :, :], light[:, :, :], tabs2_g[:, :, :], ALU.add).then_inc(s_fold, 1)
            dve.wait_ge(s_fold, 2)
            for side in range(2):
                half = light[:, side * GROUPS:(side + 1) * GROUPS, :].rearrange("p n d -> p (n d)")
                last = dve.tensor_tensor(half, half, banks[6 + side][:, :], ALU.add)
            last.then_inc(s_lmc, 1)
            dve.wait_ge(s_lmc, 6)
            dve.tensor_tensor(user_lm[:, :, :], light[:, 0:GROUPS, :], light[:, GROUPS:2 * GROUPS, :], ALU.mult).then_inc(s_lmc, 1)
            dve.wait_ge(s_lmc, 7)
            dve.tensor_reduce(gamma_id[:, :], user_lm[:, :, :], AX.X, ALU.add).then_inc(s_lmc, 1)
            dve.wait_ge(s_lmc, 8)
            dve.scalar_tensor_tensor(result[:, :], gamma_id[:, :], 0.5 / (LAYERS + 1) ** 2, gamma_lm[:, :], ALU.mult, ALU.add)\
               .then_inc(s_fin, 1)


_INS = ['r_users', 'r_items', 'L0_rec_user_emb', 'L0_rec_item_emb', 'L0_rec_rows', 'L0_rec_cols', 'L0_rec_vals',
        'L0_rec_phi3', 'L0_rec_phi4', 'L0_rec_phi2', 'L0_rec_user_lm_T', 'L0_rec_item_lm']


def kernel(**inputs):
    import numpy as _np
    import concourse.bacc as _bacc
    from concourse import mybir as _mybir
    from concourse.bass_utils import run_bass_kernel_spmd as _run

    nc = _bacc.Bacc("TRN2", target_bir_lowering=False, num_devices=1)
    arrays, args = {}, []
    for name in _INS:
        a = _np.ascontiguousarray(inputs[name])
        arrays[f"in_{name}"] = a
        args.append(nc.dram_tensor(f"in_{name}", a.shape, _mybir.dt.from_np(a.dtype), kind="ExternalInput").ap())
    batch = arrays["in_r_users"].shape[0]
    out = nc.dram_tensor("out_scores", (batch,), _mybir.dt.float32, kind="ExternalOutput").ap()
    rec_kernel(nc, *args, out)
    r = _run(nc, [arrays], core_ids=[0])
    return r.results[0]["out_scores"]
```
